# Optimizing a Trainium2 kernel written in Bass

```python
import numpy as np
import jax
import jax.numpy as jnp

def _softmax(x, axis=-1):
    return jax.nn.softmax(x, axis=axis)
def _gelu(x):
    return jax.nn.gelu(x, approximate=True)
def _silu(x):
    return jax.nn.silu(x)
def _sigmoid(x):
    return jax.nn.sigmoid(x)
def _layernorm(x, axis=-1, eps=1e-5):
    m = jnp.mean(x, axis=axis, keepdims=True)
    v = jnp.var(x, axis=axis, keepdims=True)
    return (x - m) / jnp.sqrt(v + eps)
def _scatter_add(tgt, idx, src, axis=0):
    return tgt.at[idx].add(src)
def _segment_sum(src, seg, n):
    return jax.ops.segment_sum(src, seg, n)

kernel_name = 'mk_adj_resnorm_d2_adj_128_dc43f9'

def setup_inputs(seed: int = 0):
    np.random.seed(seed)
    _w = jnp.asarray
    def _rec_inputs():
        import jax
        import jax.numpy as jnp
        _gk = jax.random.key(seed)
        x = -0.000929 + 1 * jax.random.normal(jax.random.fold_in(_gk, 1), (8192, 128), jnp.float32)
        _a = jax.random.bernoulli(jax.random.fold_in(_gk, 2), 0.00195312, (8192, 8192))
        adj = _a.astype(jnp.int32)
        return x, adj
    x, adj = _rec_inputs()
    def _L0_gnn_setup():
        import jax, jax.numpy as jnp
        import numpy as np
        NEG_BIG = -9000000000000000.0
        LEAKY_SLOPE = 0.2
        key = jax.random.key(seed)
        k1, k2, k3 = jax.random.split(key, 3)
        N, M, D = (8192, 8192, 128)
        qs = jax.random.normal(k1, (N, D), dtype=jnp.float32)
        ks = jax.random.normal(k2, (M, D), dtype=jnp.float32)
        HpGraph_e_k = jax.random.randint(k3, (N, M), 0, 2, dtype=jnp.int32)
        return {'qs': qs, 'ks': ks, 'HpGraph_e_k': HpGraph_e_k}
    _L0_gnn_all = _L0_gnn_setup()
    _L0_gnn_in = {k: v for k, v in _L0_gnn_all.items() if k in ('ks', )}
    del _L0_gnn_all

    def _L1_gnn_setup():
        import jax, jax.numpy as jnp
        import numpy as np
        NEG_INF = -9000000000000000.0
        ALPHA = 0.2
        key = jax.random.key(seed)
        k1, k2, k3, k4 = jax.random.split(key, 4)
        N, F_IN, H, D = (8192, 128, 4, 32)
        h = jax.random.normal(k1, (N, F_IN), dtype=jnp.float32)
        adj = jax.random.randint(k2, (N, N), 0, 2, dtype=jnp.int32)
        W = jax.random.normal(k3, (F_IN, H * D), dtype=jnp.float32) * (1.0 / np.sqrt(F_IN))
        a = jax.random.normal(k4, (1, H, 2 * D), dtype=jnp.float32)
        return {'h': h, 'adj': adj, 'W': W, 'a': a}
    _L1_gnn_all = _L1_gnn_setup()
    _L1_gnn_in = {k: v for k, v in _L1_gnn_all.items() if k in ('W', 'a', )}
    del _L1_gnn_all

    return {
        "x": x,
        "adj": adj,
        "L0_gnn_ks": _L0_gnn_in["ks"],
        "L1_gnn_W": _L1_gnn_in["W"],
        "L1_gnn_a": _L1_gnn_in["a"],
    }

def reference(x, adj, L0_gnn_ks, L1_gnn_W, L1_gnn_a):
    import jax
    import jax.numpy as jnp
    def _L0_gnn_ref(qs, ks, HpGraph_e_k):
        import jax, jax.numpy as jnp
        import numpy as np
        NEG_BIG = -9000000000000000.0
        LEAKY_SLOPE = 0.2
        scores = jnp.einsum('nd,md->nm', qs, ks)
        scores = jax.nn.leaky_relu(scores, negative_slope=LEAKY_SLOPE)
        scores = jnp.where(HpGraph_e_k > 0, scores, NEG_BIG)
        attn = jax.nn.softmax(scores, axis=1)
        return jnp.einsum('nm,md->nd', attn, ks)

    def _L1_gnn_ref(h, adj, W, a):
        import jax, jax.numpy as jnp
        import numpy as np
        NEG_INF = -9000000000000000.0
        ALPHA = 0.2
        N = h.shape[0]
        H = a.shape[1]
        D = a.shape[2] // 2
        Wh = (h @ W).reshape(N, H, D)
        a_src = a[0, :, :D]
        a_dst = a[0, :, D:]
        s_src = jnp.einsum('nhd,hd->nh', Wh, a_src)
        s_dst = jnp.einsum('nhd,hd->nh', Wh, a_dst)
        e = s_src[:, None, :] + s_dst[None, :, :]
        e = jnp.where(e >= 0, e, ALPHA * e)
        e = jnp.where(adj[:, :, None] > 0, e, NEG_INF)
        attention = jax.nn.softmax(e, axis=1)
        h_prime = jnp.einsum('ijh,jhd->ihd', attention, Wh)
        return jax.nn.elu(h_prime.reshape(N, H * D))

    x = _layernorm(x + _L0_gnn_ref(x, L0_gnn_ks, adj), axis=-1)
    x = _layernorm(x + _L1_gnn_ref(x, adj, L1_gnn_W, L1_gnn_a), axis=-1)
    return x


_drawn_inputs = setup_inputs


def setup_inputs(seed=0):
    import zlib

    import numpy as np

    out = dict(_drawn_inputs(seed))
    spreads = {}
    factors = {}
    for name, (base, spread) in spreads.items():
        noise = np.random.default_rng([zlib.crc32(name.encode()), seed]).standard_normal(out[name].shape)
        drawn = base * np.exp(spread * noise) if base else spread * noise
        out[name] = jnp.asarray(drawn.astype(out[name].dtype))
    for name, factor in factors.items():
        out[name] = (out[name] * factor).astype(out[name].dtype)
    return out
```

```python
from contextlib import ExitStack

import concourse.bass as bass
from concourse import mybir

ALU = mybir.AluOpType
ACT = mybir.ActivationFunctionType
F32 = mybir.dt.float32
BF16 = mybir.dt.bfloat16
I32 = mybir.dt.int32
U32 = mybir.dt.uint32
AX = mybir.AxisListType.X

P = 128
PRIMARY = 20
SLOTS = 40
SPILL = SLOTS - PRIMARY
CHUNK = 256
MASKED = -9.0e15
LEAK = 0.2
EPS = 1e-5


def adj_resnorm_kernel(nc, x, adj, ks, W, a, out):
    N, D = x.shape
    H, HD = a.shape[1], a.shape[2] // 2
    TILES = N // P
    NCH = N // CHUNK
    ROW = D + H
    EXT = D + 2 * H

    wh_dram = nc.dram_tensor("wh_rows", (N, ROW), F32, kind="Internal").ap()
    x1_dram = nc.dram_tensor("x1_rows", (N, D), F32, kind="Internal").ap()
    dst_dram = nc.dram_tensor("dst_rows", (H, N), F32, kind="Internal").ap()
    GROUPS = N // 512
    x_v = x.rearrange("(t p) d -> p t d", p=P)

    with ExitStack() as ctx:
        def sb(name, shape, dt=F32):
            return ctx.enter_context(nc.sbuf_tensor(name, shape, dt))

        def bank(name):
            return ctx.enter_context(nc.psum_tensor(name, [P, 512], F32))

        def sem(name):
            return ctx.enter_context(nc.semaphore(name))

        adj_sb = sb("adj_sb", [P, 2, N], I32)
        hit = sb("hit", [P, 2, N], BF16)
        keys = sb("keys", [P, 2, PRIMARY + 1, ROW])
        prod = sb("prod", [P, PRIMARY, D])
        prod_spill = sb("prod_spill", [P, D])
        cand = sb("cand", [P, NCH * 8])
        cand_base = sb("cand_base", [P, NCH * 8])
        cols = sb("cols", [P, 2, SLOTS])
        idx = sb("idx", [P, 2, PRIMARY + 1], U32)
        spill_end = sb("spill_end", [P, 2, 2])
        spill_n = sb("spill_n", [P, 1])
        spill_gt = sb("spill_gt", [P, SPILL])
        below_end = sb("below_end", [P, P])
        to_spill = sb("to_spill", [P, 2, P])
        to_row = sb("to_row", [P, 2, P])
        slot_of = sb("slot_of", [P, 1])
        picked = sb("picked", [P, H * SPILL])
        col_spill = sb("col_spill", [P, 1])
        spread = sb("spread", [P, H * SPILL])
        score_spill = sb("score_spill", [P, 1])
        score = sb("score", [P, SLOTS])
        e = sb("e", [P, H, SLOTS])
        prob = sb("prob", [P, 2, H, SLOTS])
        prob_spill = sb("prob_spill", [P, 2, H])
        rmax = sb("rmax", [P, H])
        neg_max = sb("neg_max", [P, 2, 1])
        rsum = sb("rsum", [P, 2, H])
        rinv = sb("rinv", [P, 2, H])
        z = sb("z", [P, 2, D])
        elu_low = sb("elu_low", [P, D])
        elu_exp = sb("elu_exp", [P, D])
        hn = sb("hn", [P, D])
        stats = sb("stats", [P, 6])
        mv = sb("mv", [P, 2, 2])
        ln_var = sb("ln_var", [P, 1])
        rstd = sb("rstd", [P, 2, 1])
        x1 = sb("x1", [P, 2, D])
        x1T = sb("x1T", [P, P])
        wh_sb = sb("wh_sb", [P, 2, EXT])
        x_sb = sb("x_sb", [P, TILES, D])
        neg_all = sb("neg_all", [P, TILES, SLOTS])
        idx_all = sb("idx_all", [P, TILES, PRIMARY + 1], U32)
        slot_all = sb("slot_all", [P, TILES, SPILL])
        end_all = sb("end_all", [P, TILES, 2])
        src_all = sb("src_all", [P, TILES, H])
        full_chunk = sb("full_chunk", [P, TILES])
        col_iota = sb("col_iota", [P, CHUNK], BF16)
        chunk_base = sb("chunk_base", [P, NCH, 8])
        pos_iota = sb("pos_iota", [P, P])
        row_iota = sb("row_iota", [P, 1])
        ident = sb("ident", [P, P])
        upper = sb("upper", [P, 2, P])
        ones = sb("ones", [P, SPILL])
        eps_sb = sb("eps_sb", [P, 1])
        w_ext = sb("w_ext", [P, EXT])
        a_sb = sb("a_sb", [P, H, 2 * HD])
        wa = sb("wa", [P, H, HD])

        bad = sb("bad", [P, 4, TILES])
        bad_n = sb("bad_n", [P, 1])
        flag = sb("flag", [1, 1], I32)
        row = hit[:, :, :].rearrange("p a n -> p (a n)").bitcast(F32)
        adj_row = adj_sb[:, 0, :]
        masked_row = adj_sb[:, 0, :].bitcast(F32)
        key_row = adj_sb[:, 1, :].bitcast(F32)
        blocks = prod[:, 0:4, :]
        turned_sb = prod[:, 4:8, :]
        acc = prod[:, 8, :]
        dst_sb = sb("dst_sb", [H, P])

        ps_end, ps_toT, ps_pick, ps_xs, ps_back, ps_pf, ps_y, ps_wh = (
            bank(n) for n in ("ps_end", "ps_toT", "ps_pick", "ps_xs", "ps_back", "ps_pf", "ps_y", "ps_wh"))

        x_in, w_in, iotas, consts, w_ready = (sem(n) for n in ("x_in", "w_in", "iotas", "consts", "w_ready"))
        adj_in = [sem("adj_in0"), sem("adj_in1")]
        gathered = [sem("gathered0"), sem("gathered1")]
        spill_gathered = [sem("spill_gathered0"), sem("spill_gathered1")]
        stored = [sem("stored0"), sem("stored1")]
        names = ("hit_ready cand_done idx_ready idx_kept spill_n_ready end_ready map_ready mapT_ready maps_done "
                 "spill_idx_ready scored spread_ready back_ready neg_max_ready prob_ready pf_ready "
                 "pf_done weighted y_ready y_read var_ready rstd_ready x1_ready x1T_ready x1T_copied wh_ready "
                 "wh_copied x1_kept").split()
        S = {n: sem(n) for n in names}
        (hit_ready, cand_done, idx_ready, idx_kept, spill_n_ready, end_ready, map_ready, mapT_ready, maps_done,
         spill_idx_ready, scored, spread_ready, back_ready, neg_max_ready, prob_ready, pf_ready,
         pf_done, weighted, y_ready, y_read, var_ready, rstd_ready, x1_ready, x1T_ready, x1T_copied, wh_ready,
         wh_copied, x1_kept) = (S[n] for n in names)
        T = {n: sem("second_" + n) for n in ("end_copied map_ready mapT_ready mapT_copied spread_ready back_ready e_ready "
                                             "prob_ready pf_ready weighted y_ready y_read low_ready exp_ready "
                                             "var_ready rstd_ready out_ready idx_copied").split()}
        gathered2 = [sem("second_gathered0"), sem("second_gathered1")]
        out_stored = [sem("out_stored0"), sem("out_stored1")]
        D0, D1 = ({n: sem(f"dense{layer}_{n}") for n in (
            "adj_in tile_in key_in values_in xT_ready xT_copied scored score_copied neg_max_ready prob_ready block_ready "
            "turned turned_copied summed added pass_done var_ready rstd_ready x1_ready x1T_ready x1T_copied "
            "wh_ready wh_copied stored low_ready exp_ready out_ready").split()} for layer in range(2))
        bad_ready, bad_summed, flag_ready = (sem(n) for n in ("bad_ready", "bad_summed", "flag_ready"))
        settled = sem("settled")
        dve_chain = sem("dve_chain")
        act_chain = sem("act_chain")

        def tiles_of(engine, step, first=4):
            with engine.Fori(0, (TILES - first) // 2) as q:
                for b in range(2):
                    step(q * 2 + (first + b), q + (first + b) // 2, b)

        def sparse(engine):
            engine.wait_ge(flag_ready, 1)
            return engine.value_load(flag[0:1, 0:1], min_val=0, max_val=1)

        def turns(engine, step):
            engine.sem_inc(settled, 1)
            with engine.Fori(0, GROUPS) as g:
                step(g)

        def dense_loads(sp):
            sp.dma_start(x_sb[:, :, :], ks.rearrange("(t p) d -> p t d", p=P)).then_inc(D0["values_in"], 16)
            with sp.Fori(0, TILES) as t:
                sp.wait_ge(D0["pass_done"], t + 1)
                sp.sem_inc(settled, 1)
                sp.dma_start(adj_row, adj[bass.ds(t * P, P), :]).then_inc(D0["adj_in"], 16)
                sp.dma_start(z[:, 0, :], x[bass.ds(t * P, P), :]).then_inc(D0["tile_in"], 16)
                sp.wait_ge(D0["wh_copied"], t + 2)
                sp.sem_inc(settled, 1)
                sp.dma_start(wh_dram[bass.ds(t * P, P), :], wh_sb[:, 0, 0:ROW]).then_inc(D0["stored"], 16)
                sp.dma_start(dst_dram[:, bass.ds(t * P, P)], dst_sb[:, :]).then_inc(D0["stored"], 16)
                sp.dma_start(x1_dram[bass.ds(t * P, P), :], x1[:, 0, :]).then_inc(D0["stored"], 16)
                sp.wait_ge(D0["stored"], t * 48 + 48)
                sp.sem_inc(settled, 1)
            sp.wait_ge(D0["pass_done"], TILES + 1)
            sp.dma_start(x_sb[:, :, :], wh_dram[:, 0:D].rearrange("(t p) d -> p t d", p=P)).then_inc(D1["values_in"], 16)
            with sp.Fori(0, TILES) as t:
                for h in range(H):
                    sp.wait_ge(D1["pass_done"], t * H + h + 1)
                    sp.sem_inc(settled, 1)
                    if h == 0:
                        sp.dma_start(z[:, 0, :], x1_dram[bass.ds(t * P, P), :]).then_inc(D1["tile_in"], 16)
                    sp.dma_start(adj_row, adj[bass.ds(t * P, P), :]).then_inc(D1["adj_in"], 16)
                    sp.dma_start(key_row, dst_dram[h:h + 1, :].to_broadcast([P, N])).then_inc(D1["key_in"], 16)
                sp.wait_ge(D1["out_ready"], t + 2)
                sp.sem_inc(settled, 1)
                sp.dma_start(out[bass.ds(t * P, P), :], x1[:, 0, :]).then_inc(D1["stored"], 16)
                sp.wait_ge(D1["stored"], t * 16 + 16)
                sp.sem_inc(settled, 1)
            sp.wait_ge(D1["stored"], 16 * TILES)

        def dense_scalar(act):
            def turn(S, src, dst, m):
                act.wait_ge(S["turned"], m + 1)
                act.activation(blocks.rearrange("p a d -> p (a d)"), src, ACT.Copy).then_inc(S["block_ready"], 1)
                act.wait_ge(S["turned"], m + 2)
                act.activation(dst, ps_toT[:, :], ACT.Copy).then_inc(S["turned_copied"], 1)

            def exp_and_turn(S, n, base):
                act.wait_ge(S["neg_max_ready"], n + 2)
                act.activation(row, row, ACT.Exp, bias=neg_max[:, 0, :],
                               accum_out=rsum[:, 0, 0:1]).then_inc(S["prob_ready"], 1)
                act.wait_ge(S["prob_ready"], n + 2)

                def values_turn(g):
                    act.wait_ge(S["summed"], n * GROUPS + g + 1)
                    turn(S, row[:, bass.ds(g * 512, 512)], turned_sb.rearrange("p a d -> p (a d)"), n * GROUPS + g + base)

                turns(act, values_turn)

            def root(S, n):
                act.wait_ge(S["var_ready"], n + 2)
                act.activation(ln_var[:, :], mv[:, 0, 1:2], ACT.Ln, bias=eps_sb[:, :]).then_inc(act_chain, 1)
                act.wait_ge(act_chain, n + (TILES + 1 + (TILES if S is D1 else 0)))
                act.activation(rstd[:, 0, :], ln_var[:, :], ACT.Exp, scale=-0.5).then_inc(S["rstd_ready"], 1)

            act.wait_ge(D0["values_in"], 16)
            turns(act, lambda g: turn(D0, x_sb[:, bass.ds(g * 4, 4), :].rearrange("p a d -> p (a d)"),
                                      key_row[:, bass.ds(g * 512, 512)], g))
            with act.Fori(0, TILES) as t:
                act.wait_ge(D0["xT_ready"], t + 2)
                act.activation(x1T[:, :], ps_wh[:, 0:P], ACT.Copy).then_inc(D0["xT_copied"], 1)
                exp_and_turn(D0, t, GROUPS)
                root(D0, t)
                act.wait_ge(D0["x1T_ready"], t + 2)
                act.activation(x1T[:, :], ps_wh[:, 0:P], ACT.Copy).then_inc(D0["x1T_copied"], 1)
                act.wait_ge(D0["wh_ready"], t + 2)
                act.activation(src_all[:, bass.ds(t, 1), :].rearrange("p a h -> p (a h)"), ps_wh[:, ROW:EXT], ACT.Copy)
                act.activation(dst_sb[:, :], ps_xs[0:H, 0:P], ACT.Copy)
                act.activation(wh_sb[:, 0, 0:ROW], ps_wh[:, 0:ROW], ACT.Copy).then_inc(D0["wh_copied"], 1)
            with act.Fori(0, TILES) as t:
                for h in range(H):
                    exp_and_turn(D1, t * H + h, 0)
                act.wait_ge(D1["low_ready"], t + 2)
                act.activation(elu_exp[:, :], elu_low[:, :], ACT.Exp).then_inc(D1["exp_ready"], 1)
                root(D1, t)

        def dense_vector(dve, restart_chain, link, at):
            def softmax_and_sum(S, n):
                link(nc.vector.scalar_tensor_tensor(row, row, LEAK, row, ALU.mult, ALU.max))
                link(nc.vector.scalar_tensor_tensor(row, adj_row, 0.0, row, ALU.is_gt, ALU.mult))
                link(nc.vector.tensor_scalar(masked_row, adj_row, 0.0, MASKED, ALU.is_le, ALU.mult))
                link(nc.vector.tensor_tensor(row, row, masked_row, ALU.add))
                link(nc.vector.tensor_reduce(rmax[:, 0:1], row, AX, ALU.max))
                nc.vector.tensor_scalar(neg_max[:, 0, :], rmax[:, 0:1], -1.0, None, ALU.mult).then_inc(S["neg_max_ready"], 1)
                link(nc.vector.memset(acc, 0.0))
                dve.wait_ge(S["prob_ready"], n + 2)
                link(nc.vector.reciprocal(rinv[:, 0, 0:1], rsum[:, 0, 0:1]))

                def add(g):
                    dve.wait_ge(S["summed"], n * GROUPS + g + 2)
                    nc.vector.tensor_tensor(acc, acc, ps_y[:, 0:D], ALU.add).then_inc(S["added"], 1)
                    dve.wait_ge(S["added"], n * GROUPS + g + 2)

                turns(dve, add)

            def norm(S, n, done):
                link(nc.vector.bn_stats(stats[:, :], z[:, 1, :]))
                nc.vector.bn_aggr(mv[:, 0, :], stats[:, :]).then_inc(S["var_ready"], 1)
                dve.wait_ge(S["rstd_ready"], n + 2)
                nc.vector.tensor_scalar(x1[:, 0, :], z[:, 1, :], mv[:, 0, 0:1], rstd[:, 0, :], ALU.subtract,
                                        ALU.mult).then_inc(done, 1)

            with dve.Fori(0, TILES) as t:
                restart_chain()

                def copy_scores(c):
                    dve.wait_ge(D0["scored"], t * GROUPS + c + 2)
                    nc.vector.tensor_copy(row[:, bass.ds(c * 512, 512)], ps_back[:, :]).then_inc(D0["score_copied"], 1)

                turns(dve, copy_scores)
                dve.wait_ge(D0["score_copied"], t * GROUPS + GROUPS + 1)
                dve.wait_ge(D0["adj_in"], t * 16 + 16)
                softmax_and_sum(D0, t)
                dve.wait_ge(D0["tile_in"], t * 16 + 16)
                link(nc.vector.scalar_tensor_tensor(z[:, 1, :], acc, rinv[:, 0, 0:1], z[:, 0, :], ALU.mult, ALU.add))
                norm(D0, t, D0["x1_ready"])
                dve.wait_ge(D0["x1T_copied"], t + 2)
                link(nc.vector.memset(score_spill[:, :], 0.0))
                nc.vector.memset(score_spill[:, :], 0.0).then_inc(D0["pass_done"], 1)
            dve.wait_ge(D0["wh_copied"], TILES + 1)
            with dve.Fori(0, TILES) as t:
                for h in range(H):
                    restart_chain()
                    n = t * H + h
                    dve.wait_ge(D1["key_in"], n * 16 + 16)
                    dve.wait_ge(D1["adj_in"], n * 16 + 16)
                    link(nc.vector.tensor_copy(spill_n[:, :], at(src_all, t)[:, h:h + 1]))
                    link(nc.vector.tensor_scalar(row, key_row, spill_n[:, :], None, ALU.add))
                    softmax_and_sum(D1, n)
                    link(nc.vector.tensor_scalar(hn[:, h * HD:(h + 1) * HD], acc[:, h * HD:(h + 1) * HD],
                                                 rinv[:, 0, 0:1], None, ALU.mult))
                    nc.vector.memset(score_spill[:, :], 0.0).then_inc(D1["pass_done"], 1)
                restart_chain()
                nc.vector.tensor_scalar(elu_low[:, :], hn[:, :], 0.0, None, ALU.min).then_inc(D1["low_ready"], 1)
                dve.wait_ge(D1["exp_ready"], t + 2)
                link(nc.vector.scalar_tensor_tensor(hn[:, :], hn[:, :], 0.0, elu_exp[:, :], ALU.max, ALU.add))
                dve.wait_ge(D1["tile_in"], t * 16 + 16)
                link(nc.vector.scalar_tensor_tensor(z[:, 1, :], hn[:, :], -1.0, z[:, 0, :], ALU.add, ALU.add))
                norm(D1, t, D1["out_ready"])
                link(nc.vector.memset(score_spill[:, :], 0.0))

        def dense_tensor(pe):
            mm = nc.tensor.matmul

            def turn(S, m):
                pe.wait_ge(S["block_ready"], m + 2)
                pe.wait_ge(S["turned_copied"], m + 1)
                for k in range(4):
                    last = nc.tensor.transpose(ps_toT[:, k * P:(k + 1) * P], blocks[:, k, :], ident[:, :])
                last.then_inc(S["turned"], 1)

            def sum_values(S, n, base):
                def group(g):
                    turn(S, n * GROUPS + g + base)
                    pe.wait_ge(S["turned_copied"], n * GROUPS + g + (base + 1) + 1)
                    pe.wait_ge(S["added"], n * GROUPS + g + 1)
                    for k in range(4):
                        last = mm(ps_y[:, 0:D], turned_sb[:, k, :],
                                  x_sb[:, bass.ds(g * 4 + k, 1), :].rearrange("p a d -> p (a d)"),
                                  start=(k == 0), stop=(k == 3))
                    last.then_inc(S["summed"], 1)

                turns(pe, group)

            turns(pe, lambda g: turn(D0, g))
            pe.wait_ge(D0["turned_copied"], GROUPS + 1)
            with pe.Fori(0, TILES) as t:
                pe.wait_ge(D0["tile_in"], t * 16 + 16)
                pe.wait_ge(D0["wh_copied"], t + 1)
                nc.tensor.transpose(ps_wh[:, 0:P], z[:, 0, :], ident[:, :]).then_inc(D0["xT_ready"], 1)
                pe.wait_ge(D0["xT_copied"], t + 2)

                def scores(c):
                    pe.wait_ge(D0["score_copied"], t * GROUPS + c + 1)
                    mm(ps_back[:, :], x1T[:, :], key_row[:, bass.ds(c * 512, 512)], start=True,
                       stop=True).then_inc(D0["scored"], 1)

                turns(pe, scores)
                sum_values(D0, t, GROUPS)
                pe.wait_ge(D0["x1_ready"], t + 2)
                nc.tensor.transpose(ps_wh[:, 0:P], x1[:, 0, :], ident[:, :]).then_inc(D0["x1T_ready"], 1)
                pe.wait_ge(D0["x1T_copied"], t + 2)
                mm(ps_xs[0:H, 0:P], w_ext[:, D:ROW], x1T[:, :], start=True, stop=True)
                mm(ps_wh[:, 0:EXT], x1T[:, :], w_ext[:, :], start=True, stop=True).then_inc(D0["wh_ready"], 1)
            pe.wait_ge(D1["values_in"], 16)
            with pe.Fori(0, TILES) as t:
                for h in range(H):
                    sum_values(D1, t * H + h, 0)

        block = ctx.enter_context(nc.Block())

        @block.sync
        def _(sp):
            sp.dma_start(x_sb[:, :, :], x_v).then_inc(x_in, 16)
            sp.dma_start(w_ext[:, 0:D], W).then_inc(w_in, 16)
            sp.dma_start(a_sb[:, :, :], a.to_broadcast([P, H, 2 * HD])).then_inc(w_in, 16)

            def load_adj(t, b):
                sp.dma_start(adj_sb[:, b, :], adj[bass.ds(t * P, P), :]).then_inc(adj_in[b], 16)

            def store_wh(t, b):
                sp.wait_ge(wh_copied, t + 1)
                sp.dma_start(wh_dram[bass.ds(t * P, P), :], wh_sb[:, b, 0:ROW]).then_inc(stored[b], 16)

            load_adj(0, 0)
            load_adj(1, 1)

            def step(t, half, b):
                sp.wait_ge(hit_ready, t - 1)
                load_adj(t, b)

            step(2, 1, 0)
            step(3, 1, 1)

            def both(t, half, b):
                step(t, half, b)
                store_wh(t - 4, b)

            tiles_of(sp, both, 4)
            for t in range(TILES - 4, TILES):
                store_wh(t, t % 2)

            with sp.If(sparse(sp) == 0):
                def store_out(t, half, b):
                    sp.wait_ge(T["out_ready"], t + 1)
                    sp.dma_start(out[bass.ds(t * P, P), :], x1[:, b, :]).then_inc(out_stored[b], 16)

                tiles_of(sp, store_out, 0)
                for b in range(2):
                    sp.wait_ge(out_stored[b], 16 * (TILES // 2))
            with sp.Else():
                dense_loads(sp)

        @block.gpsimd
        def _(pool):
            nc.gpsimd.iota(col_iota[:, :], [[1, CHUNK]], base=1, channel_multiplier=0,
                           allow_small_or_imprecise_dtypes=True).then_inc(iotas, 1)
            nc.gpsimd.iota(chunk_base[:, :, :], [[CHUNK, NCH], [0, 8]], base=0, channel_multiplier=0,
                           allow_small_or_imprecise_dtypes=True).then_inc(iotas, 1)
            nc.gpsimd.iota(pos_iota[:, :], [[1, P]], base=0, channel_multiplier=0,
                           allow_small_or_imprecise_dtypes=True).then_inc(iotas, 1)
            nc.gpsimd.iota(row_iota[:, :], [[0, 1]], base=0, channel_multiplier=1,
                           allow_small_or_imprecise_dtypes=True).then_inc(iotas, 1)

            def gather(t, half, b):
                pool.wait_ge(idx_ready, t + 1)
                if not isinstance(t, int) or t >= 2:
                    pool.wait_ge(y_ready, t - 1)
                pool.sem_inc(settled, 1)
                for s in range(PRIMARY):
                    pool.indirect_dma_start(
                        out=keys[:, b, s, 0:D], out_offset=None, in_=ks,
                        in_offset=bass.IndirectOffsetOnAxis(ap=idx[:, b, s:s + 1], axis=0)).then_inc(gathered[b], 16)
                pool.wait_ge(spill_idx_ready, t + 1)
                pool.sem_inc(settled, 1)
                pool.indirect_dma_start(
                    out=keys[:, b, PRIMARY, 0:D], out_offset=None, in_=ks,
                    in_offset=bass.IndirectOffsetOnAxis(ap=idx[:, b, PRIMARY:PRIMARY + 1], axis=0)
                ).then_inc(spill_gathered[b], 16)
                nc.gpsimd.tensor_copy(idx_all[:, bass.ds(t, 1), :].rearrange("p a n -> p (a n)"), idx[:, b, :]).then_inc(idx_kept, 1)

            gather(0, 0, 0)
            gather(1, 0, 1)
            tiles_of(pool, gather, 2)

            with pool.If(sparse(pool) == 0):
                for b in range(2):
                    pool.wait_ge(stored[b], 16 * (TILES // 2))
                pool.wait_ge(idx_kept, TILES)
                pool.wait_ge(y_ready, TILES)

                def gather2(t, half, b):
                    nc.gpsimd.tensor_copy(idx[:, b, :], idx_all[:, bass.ds(t, 1), :].rearrange("p a n -> p (a n)")).then_inc(T["idx_copied"], 1)
                    pool.wait_ge(T["idx_copied"], t + 1)
                    if not isinstance(t, int) or t >= 2:
                        pool.wait_ge(T["y_ready"], t - 1)
                    pool.sem_inc(settled, 1)
                    for s in range(PRIMARY + 1):
                        pool.indirect_dma_start(
                            out=keys[:, b, s, :], out_offset=None, in_=wh_dram,
                            in_offset=bass.IndirectOffsetOnAxis(ap=idx[:, b, s:s + 1], axis=0)).then_inc(gathered2[b], 16)

                def gather2_free(t, half, b):
                    pool.wait_ge(gathered2[b], 336 * half)
                    gather2(t, half, b)

                gather2(0, 0, 0)
                gather2(1, 0, 1)
                tiles_of(pool, gather2_free, 2)
            with pool.Else():
                pool.wait_ge(flag_ready, 1)

        @block.scalar
        def _(act):
            def sign(t, half, b):
                act.wait_ge(adj_in[b], half * 16 + 16)
                if not isinstance(t, int) or t >= 2:
                    act.wait_ge(cand_done, t - 1)
                act.activation(hit[:, b, :], adj_sb[:, b, :], ACT.Sign).then_inc(hit_ready, 1)

            def finish(t, half, b):
                act.wait_ge(var_ready, t + 1)
                act.activation(ln_var[:, :], mv[:, b, 1:2], ACT.Ln, bias=eps_sb[:, :]).then_inc(act_chain, 1)
                act.wait_ge(act_chain, t + 1)
                act.activation(rstd[:, b, :], ln_var[:, :], ACT.Exp, scale=-0.5).then_inc(rstd_ready, 1)
                act.wait_ge(x1_ready, t + 1)
                act.activation(x_sb[:, bass.ds(t, 1), :].rearrange("p a d -> p (a d)"), x1[:, b, :], ACT.Copy).then_inc(x1_kept, 1)
                act.wait_ge(x1T_ready, t + 1)
                act.activation(x1T[:, :], ps_wh[:, 0:P], ACT.Copy).then_inc(x1T_copied, 1)
                act.wait_ge(wh_ready, t + 1)
                if not isinstance(t, int) or t >= 2:
                    act.wait_ge(stored[b], half * 16)
                act.activation(src_all[:, bass.ds(t, 1), :].rearrange("p a h -> p (a h)"), ps_wh[:, ROW:EXT], ACT.Copy)
                act.activation(wh_sb[:, b, 0:ROW], ps_wh[:, 0:ROW], ACT.Copy).then_inc(wh_copied, 1)

            def softmax(t, half, b):
                act.wait_ge(neg_max_ready, t + 1)
                act.activation(prob[:, b, 0, :], score[:, :], ACT.Exp, bias=neg_max[:, b, :],
                               accum_out=rsum[:, b, 0:1]).then_inc(prob_ready, 1)

            def copy_map(t, half, b):
                act.wait_ge(mapT_ready, t + 1)
                act.activation(to_row[:, b, :], ps_toT[:, 0:P], ACT.Copy).then_inc(maps_done, 1)

            def weigh(t, half, b):
                act.wait_ge(prob_ready, t + 1)
                act.wait_ge(scored, t + 1)
                for s in range(PRIMARY):
                    act.activation(keys[:, b, s, 0:D], keys[:, b, s, 0:D], ACT.Copy, scale=prob[:, b, 0, s:s + 1])
                act.wait_ge(pf_done, t + 1)
                act.activation(keys[:, b, PRIMARY, 0:D], keys[:, b, PRIMARY, 0:D], ACT.Copy,
                               scale=prob_spill[:, b, 0:1]).then_inc(weighted, 1)

            def step(t, half, b, lists=True, attend=True, end=True):
                if lists and not (isinstance(t, int) and t == TILES - 1):
                    sign(t + 1, half + b, 1 - b)
                if end:
                    finish(t - 2, half - 1, b)
                if attend:
                    softmax(t - 1, half - 1 + b, 1 - b)
                if lists:
                    copy_map(t, half, b)
                if attend:
                    weigh(t - 1, half - 1 + b, 1 - b)

            act.wait_ge(consts, 1)
            sign(0, 0, 0)
            step(0, 0, 0, attend=False, end=False)
            step(1, 0, 1, end=False)
            step(2, 1, 0)
            step(3, 1, 1)
            with act.Fori(0, (TILES - 6) // 2) as q:
                for b in range(2):
                    step(q * 2 + (4 + b), q + 2, b)
            step(TILES - 2, TILES // 2 - 1, 0)
            step(TILES - 1, TILES // 2 - 1, 1)
            step(TILES, TILES // 2, 0, lists=False)
            finish(TILES - 1, TILES // 2 - 1, 1)

            with act.If(sparse(act) == 0):
                def copy_ends(t, half, b):
                    act.activation(spill_end[:, b, :], end_all[:, bass.ds(t, 1), :].rearrange("p a n -> p (a n)"), ACT.Copy).then_inc(T["end_copied"], 1)

                def copy_map2(t, half, b):
                    act.wait_ge(T["mapT_ready"], t + 1)
                    act.activation(to_row[:, b, :], ps_toT[:, 0:P], ACT.Copy).then_inc(T["mapT_copied"], 1)

                def softmax2(t, half, b):
                    act.wait_ge(T["e_ready"], t + 1)
                    act.activation(prob[:, b, :, :], e[:, :, :], ACT.Exp).then_inc(T["prob_ready"], 1)

                def finish2(t, half, b):
                    act.wait_ge(T["low_ready"], t + 1)
                    act.activation(elu_exp[:, :], elu_low[:, :], ACT.Exp).then_inc(T["exp_ready"], 1)
                    act.wait_ge(T["var_ready"], t + 1)
                    act.activation(ln_var[:, :], mv[:, b, 1:2], ACT.Ln, bias=eps_sb[:, :]).then_inc(act_chain, 1)
                    act.wait_ge(act_chain, t + (TILES + 1))
                    act.activation(rstd[:, b, :], ln_var[:, :], ACT.Exp, scale=-0.5).then_inc(T["rstd_ready"], 1)

                def step2(t, half, b, maps=True, attend=True, end=True):
                    if maps:
                        if not isinstance(t, int) or t >= 2:
                            act.wait_ge(T["map_ready"], t - 1)
                        copy_ends(t, half, b)
                        copy_map2(t, half, b)
                    if attend:
                        softmax2(t - 1, half - 1 + b, 1 - b)
                    if end:
                        finish2(t - 2, half - 1, b)

                step2(0, 0, 0, attend=False, end=False)
                step2(1, 0, 1, end=False)
                step2(2, 1, 0)
                step2(3, 1, 1)
                tiles_of(act, step2)
                step2(TILES, TILES // 2, 0, maps=False)
                finish2(TILES - 1, TILES // 2 - 1, 1)
            with act.Else():
                dense_scalar(act)

        @block.vector
        def _(dve):
            count = [0]

            def restart_chain():
                dve.sem_clear(dve_chain)
                count[0] = 0

            def link(ins):
                count[0] += 1
                ins.then_inc(dve_chain, 1)
                dve.wait_ge(dve_chain, count[0])

            def at(buf, t):
                return buf[:, bass.ds(t, 1), :].rearrange("p a n -> p (a n)")

            def spread_over(ap, n, d):
                return ap.rearrange("p (a d) -> p a d", a=1).to_broadcast([P, n, d])

            def each(ap, n, d):
                return ap.rearrange("p (n a) -> p n a", a=1).to_broadcast([P, n, d])

            nc.vector.memset(ones[:, :], 1.0)
            nc.vector.memset(eps_sb[:, :], EPS)
            dve.wait_ge(iotas, 4)
            link(nc.vector.tensor_scalar(ident[:, :], pos_iota[:, :], row_iota[:, 0:1], None, ALU.is_equal))
            link(nc.vector.tensor_scalar(upper[:, 0, :], pos_iota[:, :], row_iota[:, 0:1], None, ALU.is_gt))
            link(nc.vector.tensor_scalar(upper[:, 1, :], pos_iota[:, :], row_iota[:, 0:1], None, ALU.is_ge))
            nc.vector.memset(score_spill[:, :], 0.0).then_inc(consts, 1)
            dve.wait_ge(w_in, 32)
            for k, lo in ((0, HD), (1, 0)):
                link(nc.vector.tensor_tensor(wa[:, :, :], w_ext[:, 0:D].rearrange("p (h k) -> p h k", h=H),
                                             a_sb[:, :, lo:lo + HD], ALU.mult))
                link(nc.vector.tensor_reduce(w_ext[:, D + k * H:D + (k + 1) * H], wa[:, :, :], AX, ALU.add))
            nc.vector.memset(score_spill[:, :], 0.0).then_inc(w_ready, 1)
            dve.wait_ge(x_in, 16)

            def candidates(t, half, b):
                dve.wait_ge(hit_ready, t + 1)
                view = hit[:, b, :].rearrange("p (c n) -> p c n", n=CHUNK)
                link(nc.vector.tensor_tensor(view, view, spread_over(col_iota[:, :], NCH, CHUNK), ALU.mult))
                for c in range(NCH):
                    last = nc.vector.max(cand[:, 8 * c:8 * c + 8], hit[:, b, c * CHUNK:(c + 1) * CHUNK])
                last.then_inc(cand_done, 1)
                dve.wait_ge(cand_done, t + 1)
                link(nc.vector.tensor_reduce(full_chunk[:, bass.ds(t, 1)],
                                             cand[:, :].rearrange("p (c k) -> p c k", k=8)[:, :, 7], AX, ALU.max))

            def lists(t, half, b):
                link(nc.vector.scalar_tensor_tensor(cand_base[:, :], cand[:, :], 0.0,
                                                    chunk_base[:, :, :].rearrange("p c k -> p (c k)"),
                                                    ALU.is_gt, ALU.mult))
                link(nc.vector.scalar_tensor_tensor(cand[:, :], cand[:, :], 0.0, cand_base[:, :], ALU.max, ALU.add))
                for r in range(0, SLOTS, 8):
                    link(nc.vector.max(cols[:, b, r:r + 8], cand[:, :]))
                    if r + 8 < SLOTS:
                        link(nc.vector.match_replace(cand[:, :], cols[:, b, r:r + 8], cand[:, :], 0.0))
                nc.vector.scalar_tensor_tensor(spill_gt[:, :], cols[:, b, PRIMARY:SLOTS], 0.0, ones[:, :], ALU.is_gt,
                                               ALU.mult, accum_out=spill_n[:, :]).then_inc(spill_n_ready, 1)
                if not isinstance(t, int) or t >= 2:
                    dve.wait_ge(idx_kept, t - 1)
                    dve.wait_ge(gathered[b], half * (16 * PRIMARY))
                    dve.wait_ge(spill_gathered[b], half * 16)
                nc.vector.tensor_scalar(idx[:, b, 0:PRIMARY], cols[:, b, 0:PRIMARY], -1.0, 0.0, ALU.add,
                                        ALU.max).then_inc(idx_ready, 1)
                link(nc.vector.tensor_scalar(at(neg_all, t), cols[:, b, :], 0.0, MASKED, ALU.is_le, ALU.mult))

            def spill_map(t, half, b):
                dve.wait_ge(end_ready, t + 1)
                link(nc.vector.tensor_copy(spill_end[:, b, :], ps_end[:, 0:2]))
                link(nc.vector.tensor_copy(at(end_all, t), spill_end[:, b, :]))
                make_map(b).then_inc(map_ready, 1)

            def make_map(b):
                link(nc.vector.tensor_scalar(below_end[:, :], pos_iota[:, :], spill_end[:, b, 1:2], None, ALU.is_lt))
                return nc.vector.scalar_tensor_tensor(to_spill[:, b, :], pos_iota[:, :], spill_end[:, b, 0:1],
                                                      below_end[:, :], ALU.is_ge, ALU.mult)

            def spill_idx(t, half, b):
                dve.wait_ge(mapT_ready, t + 1)
                link(nc.vector.scalar_tensor_tensor(slot_of[:, :], ps_pick[:, SPILL:SPILL + 1], -1.0,
                                                    row_iota[:, :], ALU.mult, ALU.add))
                link(nc.vector.tensor_scalar(at(slot_all, t), pos_iota[:, 0:SPILL], slot_of[:, 0:1], None, ALU.is_equal))
                link(nc.vector.scalar_tensor_tensor(picked[:, 0:SPILL], pos_iota[:, 0:SPILL], slot_of[:, 0:1],
                                                    ps_pick[:, 0:SPILL], ALU.is_equal, ALU.mult,
                                                    accum_out=col_spill[:, :]))
                nc.vector.tensor_scalar(idx[:, b, PRIMARY:PRIMARY + 1], col_spill[:, :], -1.0, 0.0, ALU.add,
                                        ALU.max).then_inc(spill_idx_ready, 1)

            def dots(t, half, b):
                dve.wait_ge(gathered[b], half * (16 * PRIMARY) + 16 * PRIMARY)
                link(nc.vector.tensor_tensor(prod[:, :, :], keys[:, b, 0:PRIMARY, 0:D],
                                             spread_over(at(x_sb, t), PRIMARY, D), ALU.mult))
                link(nc.vector.tensor_reduce(score[:, 0:PRIMARY], prod[:, :, :], AX, ALU.add))
                dve.wait_ge(spill_gathered[b], half * 16 + 16)
                link(nc.vector.scalar_tensor_tensor(prod_spill[:, :], keys[:, b, PRIMARY, 0:D], 1.0, ps_xs[:, 0:D],
                                                    ALU.mult, ALU.mult, accum_out=score_spill[:, :]))
                nc.vector.tensor_scalar(spread[:, 0:SPILL], at(slot_all, t), score_spill[:, 0:1], None,
                                        ALU.mult).then_inc(scored, 1)

            def maxima(t, half, b):
                dve.wait_ge(back_ready, t + 1)
                link(nc.vector.tensor_copy(score[:, PRIMARY:SLOTS], ps_back[:, 0:SPILL]))
                link(nc.vector.tensor_tensor(score[:, :], score[:, :], at(neg_all, t), ALU.add))
                link(nc.vector.scalar_tensor_tensor(score[:, :], score[:, :], LEAK, score[:, :], ALU.mult, ALU.max))
                link(nc.vector.tensor_reduce(rmax[:, 0:1], score[:, :], AX, ALU.max))
                nc.vector.tensor_scalar(neg_max[:, b, :], rmax[:, 0:1], -1.0, None, ALU.mult).then_inc(neg_max_ready, 1)

            def spill_prob(t, half, b):
                dve.wait_ge(pf_ready, t + 1)
                link(nc.vector.scalar_tensor_tensor(picked[:, 0:SPILL], at(slot_all, t), 1.0, ps_pf[:, 0:SPILL],
                                                    ALU.mult, ALU.mult, accum_out=prob_spill[:, b, 0:1]))
                nc.vector.reciprocal(rinv[:, b, 0:1], rsum[:, b, 0:1]).then_inc(pf_done, 1)

            def norm_stats(zb, b):
                link(nc.vector.bn_stats(stats[:, :], zb))
                return nc.vector.bn_aggr(mv[:, b, :], stats[:, :])

            def norm_a(t, half, b):
                dve.wait_ge(y_ready, t + 1)
                link(nc.vector.scalar_tensor_tensor(z[:, b, :], ps_y[:, 0:D], rinv[:, b, 0:1], at(x_sb, t),
                                                    ALU.mult, ALU.add))
                norm_stats(z[:, b, :], b).then_inc(var_ready, 1)

            def norm_b(t, half, b):
                dve.wait_ge(rstd_ready, t + 1)
                if not isinstance(t, int) or t >= 2:
                    dve.wait_ge(x1_kept, t - 1)
                nc.vector.tensor_scalar(x1[:, b, :], z[:, b, :], mv[:, b, 0:1], rstd[:, b, :], ALU.subtract,
                                        ALU.mult).then_inc(x1_ready, 1)

            def step(t, half, b, lst=True, attend=True, end=True):
                restart_chain()
                prev = (t - 1, half - 1 + b, 1 - b)
                if lst:
                    candidates(t, half, b)
                if end:
                    norm_a(t - 2, half - 1, b)
                if attend:
                    dots(*prev)
                if end:
                    norm_b(t - 2, half - 1, b)
                if lst:
                    lists(t, half, b)
                if attend:
                    maxima(*prev)
                if lst:
                    spill_map(t, half, b)
                if attend:
                    spill_prob(*prev)
                if lst:
                    spill_idx(t, half, b)
                link(nc.vector.memset(score_spill[:, :], 0.0))

            step(0, 0, 0, attend=False, end=False)
            step(1, 0, 1, end=False)
            step(2, 1, 0)
            step(3, 1, 1)
            tiles_of(dve, step)
            step(TILES, TILES // 2, 0, lst=False)
            restart_chain()
            norm_a(TILES - 1, TILES // 2 - 1, 1)
            norm_b(TILES - 1, TILES // 2 - 1, 1)
            link(nc.vector.memset(score_spill[:, :], 0.0))

            restart_chain()
            link(nc.vector.tensor_scalar(bad[:, 0, :], neg_all[:, :, 0], -1.0, None, ALU.is_lt))
            link(nc.vector.tensor_scalar(bad[:, 1, :], neg_all[:, :, SLOTS - 1], -1.0, None, ALU.is_gt))
            link(nc.vector.tensor_scalar(bad[:, 2, :], full_chunk[:, :], 0.0, None, ALU.is_gt))
            link(nc.vector.tensor_scalar(bad[:, 3, :], end_all[:, :, 1], float(P), None, ALU.is_gt))
            link(nc.vector.tensor_reduce(bad_n[:, :], bad[:, :, :].rearrange("p k t -> p (k t)"), AX, ALU.add))
            nc.vector.memset(score_spill[:, :], 0.0).then_inc(bad_ready, 1)
            for S in (D0, D1):
                for name in S:
                    if not name.endswith("_in") and name != "stored":
                        dve.sem_inc(S[name], 1)
            dve.wait_ge(bad_summed, 1)
            nc.vector.tensor_scalar(flag[:, :], ps_end[0:1, 0:1], 1.0, None, ALU.min).then_inc(flag_ready, 1)

            with dve.If(sparse(dve) == 0):
                def maps2(t, half, b):
                    dve.wait_ge(T["end_copied"], t + 1)
                    make_map(b).then_inc(T["map_ready"], 1)

                def scores2a(t, half, b):
                    dve.wait_ge(gathered2[b], half * 336 + 336)
                    nc.vector.tensor_tensor(
                        spread[:, :].rearrange("p (h s) -> p h s", h=H), spread_over(at(slot_all, t), H, SPILL),
                        each(keys[:, b, PRIMARY, D:ROW], H, SPILL), ALU.mult).then_inc(T["spread_ready"], 1)
                    link(nc.vector.tensor_tensor(e[:, :, 0:PRIMARY],
                                                 keys[:, b, 0:PRIMARY, D:ROW].rearrange("p s h -> p h s"),
                                                 each(at(src_all, t), H, PRIMARY), ALU.add))

                def scores2b(t, half, b):
                    dve.wait_ge(T["back_ready"], t + 1)
                    link(nc.vector.tensor_tensor(e[:, :, PRIMARY:SLOTS],
                                                 ps_back[:, 0:H * SPILL].rearrange("p (h s) -> p h s", h=H),
                                                 each(at(src_all, t), H, SPILL), ALU.add))
                    link(nc.vector.tensor_tensor(e[:, :, :], e[:, :, :], spread_over(at(neg_all, t), H, SLOTS), ALU.add))
                    flat = e[:, :, :].rearrange("p h s -> p (h s)")
                    link(nc.vector.scalar_tensor_tensor(flat, flat, LEAK, flat, ALU.mult, ALU.max))
                    link(nc.vector.tensor_reduce(rmax[:, :], e[:, :, :], AX, ALU.max))
                    nc.vector.tensor_tensor(e[:, :, :], e[:, :, :], each(rmax[:, :], H, SLOTS),
                                            ALU.subtract).then_inc(T["e_ready"], 1)

                def weigh2(t, half, b):
                    dve.wait_ge(T["prob_ready"], t + 1)
                    by_head = keys[:, b, 0:PRIMARY, 0:D].rearrange("p s (h k) -> p s h k", h=H)
                    nc.vector.tensor_tensor(
                        by_head, by_head,
                        prob[:, b, :, 0:PRIMARY].rearrange("p h (s a) -> p s h a", a=1).to_broadcast([P, PRIMARY, H, HD]),
                        ALU.mult)
                    link(nc.vector.tensor_reduce(rsum[:, b, :], prob[:, b, :, :], AX, ALU.add))
                    link(nc.vector.reciprocal(rinv[:, b, :], rsum[:, b, :]))
                    dve.wait_ge(T["pf_ready"], t + 1)
                    link(nc.vector.tensor_tensor(picked[:, :].rearrange("p (h s) -> p h s", h=H),
                                                 ps_pf[:, 0:H * SPILL].rearrange("p (h s) -> p h s", h=H),
                                                 spread_over(at(slot_all, t), H, SPILL), ALU.mult))
                    link(nc.vector.tensor_reduce(prob_spill[:, b, :], picked[:, :].rearrange("p (h s) -> p h s", h=H),
                                                 AX, ALU.add))
                    spill = keys[:, b, PRIMARY, 0:D].rearrange("p (h k) -> p h k", h=H)
                    nc.vector.tensor_tensor(spill, spill, each(prob_spill[:, b, :], H, HD),
                                            ALU.mult).then_inc(T["weighted"], 1)

                def norm2_a(t, half, b):
                    dve.wait_ge(T["y_ready"], t + 1)
                    link(nc.vector.tensor_tensor(hn[:, :].rearrange("p (h k) -> p h k", h=H),
                                                 ps_y[:, 0:D].rearrange("p (h k) -> p h k", h=H),
                                                 each(rinv[:, b, :], H, HD), ALU.mult))
                    nc.vector.tensor_scalar(elu_low[:, :], hn[:, :], 0.0, None, ALU.min).then_inc(T["low_ready"], 1)

                def norm2_b(t, half, b):
                    dve.wait_ge(T["exp_ready"], t + 1)
                    link(nc.vector.scalar_tensor_tensor(hn[:, :], hn[:, :], 0.0, elu_exp[:, :], ALU.max, ALU.add))
                    link(nc.vector.scalar_tensor_tensor(z[:, b, :], hn[:, :], -1.0, at(x_sb, t), ALU.add, ALU.add))
                    norm_stats(z[:, b, :], b).then_inc(T["var_ready"], 1)
                    dve.wait_ge(T["rstd_ready"], t + 1)
                    if not isinstance(t, int) or t >= 2:
                        dve.wait_ge(out_stored[b], half * 16)
                    nc.vector.tensor_scalar(x1[:, b, :], z[:, b, :], mv[:, b, 0:1], rstd[:, b, :], ALU.subtract,
                                            ALU.mult).then_inc(T["out_ready"], 1)

                def step2(t, half, b, maps=True, attend=True, end=True):
                    restart_chain()
                    prev = (t - 1, half - 1 + b, 1 - b)
                    if maps:
                        maps2(t, half, b)
                    if attend:
                        scores2a(*prev)
                    if end:
                        norm2_a(t - 2, half - 1, b)
                    if attend:
                        scores2b(*prev)
                    if end:
                        norm2_b(t - 2, half - 1, b)
                    if attend:
                        weigh2(*prev)
                    link(nc.vector.memset(score_spill[:, :], 0.0))

                dve.wait_ge(x1_kept, TILES)
                dve.wait_ge(wh_copied, TILES)
                step2(0, 0, 0, attend=False, end=False)
                step2(1, 0, 1, end=False)
                step2(2, 1, 0)
                step2(3, 1, 1)
                tiles_of(dve, step2)
                step2(TILES, TILES // 2, 0, maps=False)
                restart_chain()
                norm2_a(TILES - 1, TILES // 2 - 1, 1)
                norm2_b(TILES - 1, TILES // 2 - 1, 1)
            with dve.Else():
                dense_vector(dve, restart_chain, link, at)

        @block.tensor
        def _(pe):
            mm = nc.tensor.matmul

            def finish(t, half, b):
                pe.wait_ge(x1_ready, t + 1)
                if not isinstance(t, int) or t >= 1:
                    pe.wait_ge(wh_copied, t)
                nc.tensor.transpose(ps_wh[:, 0:P], x1[:, b, :], ident[:, :]).then_inc(x1T_ready, 1)
                pe.wait_ge(x1T_copied, t + 1)
                mm(ps_wh[:, 0:EXT], x1T[:, :], w_ext[:, :], start=True, stop=True).then_inc(wh_ready, 1)

            def back(t, half, b):
                pe.wait_ge(scored, t + 1)
                pe.wait_ge(maps_done, t + 1)
                mm(ps_back[:, 0:SPILL], to_row[:, b, :], spread[:, 0:SPILL], start=True, stop=True).then_inc(back_ready, 1)

            def ends(t, half, b):
                pe.wait_ge(spill_n_ready, t + 1)
                mm(ps_end[:, 0:1], upper[:, 0, :], spill_n[:, :], start=True, stop=True)
                mm(ps_end[:, 1:2], upper[:, 1, :], spill_n[:, :], start=True, stop=True).then_inc(end_ready, 1)

            def maps(t, half, b):
                pe.wait_ge(map_ready, t + 1)
                mm(ps_pick[:, 0:SPILL], to_spill[:, b, :], cols[:, b, PRIMARY:SLOTS], start=True, stop=True)
                mm(ps_pick[:, SPILL:SPILL + 1], to_spill[:, b, :], spill_end[:, b, 0:1], start=True, stop=True)
                mm(ps_xs[:, 0:D], to_spill[:, b, :], x_sb[:, bass.ds(t, 1), :].rearrange("p a d -> p (a d)"),
                   start=True, stop=True)
                nc.tensor.transpose(ps_toT[:, 0:P], to_spill[:, b, :], ident[:, :]).then_inc(mapT_ready, 1)

            def probs(t, half, b):
                pe.wait_ge(prob_ready, t + 1)
                mm(ps_pf[:, 0:SPILL], to_spill[:, b, :], prob[:, b, 0, PRIMARY:SLOTS], start=True,
                   stop=True).then_inc(pf_ready, 1)

            def sum_rows(b, done):
                for s in range(PRIMARY):
                    mm(ps_y[:, 0:D], ident[:, :], keys[:, b, s, 0:D], start=(s == 0), stop=False)
                mm(ps_y[:, 0:D], to_row[:, b, :], keys[:, b, PRIMARY, 0:D], start=False, stop=True).then_inc(done, 1)

            def weighted_sum(t, half, b):
                pe.wait_ge(weighted, t + 1)
                if not isinstance(t, int) or t >= 1:
                    pe.wait_ge(var_ready, t)
                sum_rows(b, y_ready)

            def step(t, half, b, lst=True, attend=True, end=True):
                prev = (t - 1, half - 1 + b, 1 - b)
                if end:
                    finish(t - 2, half - 1, b)
                if attend:
                    back(*prev)
                if lst:
                    ends(t, half, b)
                    maps(t, half, b)
                if attend:
                    probs(*prev)
                    weighted_sum(*prev)

            pe.wait_ge(consts, 1)
            pe.wait_ge(w_ready, 1)
            pe.wait_ge(x_in, 16)
            step(0, 0, 0, attend=False, end=False)
            step(1, 0, 1, end=False)
            step(2, 1, 0)
            step(3, 1, 1)
            tiles_of(pe, step)
            step(TILES, TILES // 2, 0, lst=False)
            finish(TILES - 1, TILES // 2 - 1, 1)

            pe.wait_ge(bad_ready, 1)
            mm(ps_end[0:1, 0:1], bad_n[:, :], ones[:, 0:1], start=True, stop=True).then_inc(bad_summed, 1)

            with pe.If(sparse(pe) == 0):
                def maps2(t, half, b):
                    pe.wait_ge(T["map_ready"], t + 1)
                    if not isinstance(t, int) or t >= 1:
                        pe.wait_ge(T["mapT_copied"], t)
                    nc.tensor.transpose(ps_toT[:, 0:P], to_spill[:, b, :], ident[:, :]).then_inc(T["mapT_ready"], 1)

                def back2(t, half, b):
                    pe.wait_ge(T["spread_ready"], t + 1)
                    pe.wait_ge(T["mapT_copied"], t + 1)
                    mm(ps_back[:, 0:H * SPILL], to_row[:, b, :], spread[:, :], start=True, stop=True).then_inc(T["back_ready"], 1)

                def probs2(t, half, b):
                    pe.wait_ge(T["prob_ready"], t + 1)
                    mm(ps_pf[:, 0:H * SPILL], to_spill[:, b, :], prob[:, b, :, PRIMARY:SLOTS], start=True,
                       stop=True).then_inc(T["pf_ready"], 1)

                def step2(t, half, b, maps=True, attend=True, end=True):
                    prev = (t - 1, half - 1 + b, 1 - b)
                    if maps:
                        maps2(t, half, b)
                    if attend:
                        back2(*prev)
                        probs2(*prev)
                        pe.wait_ge(T["weighted"], prev[0] + 1)
                        if not isinstance(t, int) or t >= 2:
                            pe.wait_ge(T["low_ready"], t - 1)
                        sum_rows(1 - b, T["y_ready"])

                step2(0, 0, 0, attend=False)
                step2(1, 0, 1)
                step2(2, 1, 0)
                step2(3, 1, 1)
                tiles_of(pe, step2)
                step2(TILES, TILES // 2, 0, maps=False)
            with pe.Else():
                dense_tensor(pe)

_INS = ["x", "adj", "L0_gnn_ks", "L1_gnn_W", "L1_gnn_a"]


def kernel(**inputs):
    import numpy as np
    import concourse.bacc as bacc
    from concourse.bass_utils import run_bass_kernel_spmd as run

    nc = bacc.Bacc("TRN2", target_bir_lowering=False, num_devices=1)
    arrays, args = {}, []
    for name in _INS:
        v = np.ascontiguousarray(inputs[name])
        arrays[f"in_{name}_dram"] = v
        args.append(nc.dram_tensor(f"in_{name}_dram", v.shape, mybir.dt.from_np(v.dtype), kind="ExternalInput").ap())
    out = nc.dram_tensor("out_dram", inputs["x"].shape, F32, kind="ExternalOutput").ap()
    adj_resnorm_kernel(nc, *args, out)
    return run(nc, [arrays], core_ids=[0]).results[0]["out_dram"]
```

```python
from contextlib import ExitStack

import concourse.bass as bass
from concourse import mybir

ALU = mybir.AluOpType
ACT = mybir.ActivationFunctionType
F32 = mybir.dt.float32
BF16 = mybir.dt.bfloat16
I32 = mybir.dt.int32
U32 = mybir.dt.uint32
AX = mybir.AxisListType.X

P = 128
PRIMARY = 19
EARLY = 9
SLOTS = 40
SPILL = SLOTS - PRIMARY
FOLD = 8
CHUNK = 64
MASKED = -9.0e15
LEAK = 0.2
EPS = 1e-5


def adj_resnorm_kernel(nc, x, adj, ks, W, a, out):
    N, D = x.shape
    H, HD = a.shape[1], a.shape[2] // 2
    TILES = N // P
    POS = N // FOLD
    NCH = POS // CHUNK
    ROW = D + H
    EXT = D + 2 * H

    wh_dram = nc.dram_tensor("wh_rows", (N, ROW), F32, kind="Internal").ap()
    x1_dram = nc.dram_tensor("x1_rows", (N, D), F32, kind="Internal").ap()
    dst_dram = nc.dram_tensor("dst_rows", (H, N), F32, kind="Internal").ap()
    GROUPS = N // 512
    x_v = x.rearrange("(t p) d -> p t d", p=P)

    with ExitStack() as ctx:
        def sb(name, shape, dt=F32):
            return ctx.enter_context(nc.sbuf_tensor(name, shape, dt))

        def bank(name):
            return ctx.enter_context(nc.psum_tensor(name, [P, 512], F32))

        def sem(name):
            return ctx.enter_context(nc.semaphore(name))

        adj_sb = sb("adj_sb", [P, 2, N], I32)
        hit = sb("hit", [P, 2, N], BF16)
        keys = sb("keys", [P, 2, PRIMARY + 1, ROW])
        weighed = sb("weighed", [P, PRIMARY + 1, D])
        prod = sb("prod", [P, 4, D])
        cand = sb("cand", [P, NCH * 8])
        codes = sb("codes", [P, SLOTS])
        code_int = sb("code_int", [P, SLOTS], I32)
        grid_bits = sb("grid_bits", [P, FOLD, SLOTS], I32)
        grid_cols = sb("grid_cols", [P, FOLD, SLOTS], I32)
        grid = sb("grid", [P, FOLD, SLOTS])
        cols = sb("cols", [P, 2, SLOTS])
        idx = sb("idx", [P, 2, PRIMARY + 1], U32)
        spill_end = sb("spill_end", [P, 2, 2])
        spill_n = sb("spill_n", [P, 1])
        spill_gt = sb("spill_gt", [P, SPILL])
        below_end = sb("below_end", [P, P])
        to_spill = sb("to_spill", [P, 2, P])
        to_row = sb("to_row", [P, 2, P])
        slot_of = sb("slot_of", [P, 1])
        picked = sb("picked", [P, H * SPILL])
        col_spill = sb("col_spill", [P, 1])
        spread = sb("spread", [P, H * SPILL])
        score_spill = sb("score_spill", [P, 1])
        score = sb("score", [P, SLOTS])
        e = sb("e", [P, H, SLOTS])
        prob = sb("prob", [P, 2, H, SLOTS])
        prob_spill = sb("prob_spill", [P, 2, H])
        rmax = sb("rmax", [P, H])
        neg_max = sb("neg_max", [P, 2, 1])
        rsum = sb("rsum", [P, 2, H])
        rinv = sb("rinv", [P, 2, H])
        z = sb("z", [P, 2, D])
        elu_low = sb("elu_low", [P, D])
        elu_exp = sb("elu_exp", [P, D])
        hn = sb("hn", [P, D])
        stats = sb("stats", [P, 6])
        mv = sb("mv", [P, 2, 2])
        ln_var = sb("ln_var", [P, 1])
        rstd = sb("rstd", [P, 2, 1])
        x1 = sb("x1", [P, 2, D])
        x1T = sb("x1T", [P, P])
        wh_sb = sb("wh_sb", [P, 2, EXT])
        x_sb = sb("x_sb", [P, TILES, D])
        neg_all = sb("neg_all", [P, TILES, SLOTS])
        idx_all = sb("idx_all", [P, TILES, PRIMARY + 1], U32)
        slot_all = sb("slot_all", [P, TILES, SPILL])
        end_all = sb("end_all", [P, TILES, 2])
        src_all = sb("src_all", [P, TILES, H])
        edge_sum = sb("edge_sum", [P, TILES])
        pos_high = sb("pos_high", [P, POS // 256], BF16)
        pos_low = sb("pos_low", [P, 256], BF16)
        scaled_id = sb("scaled_id", [P, FOLD + 2, P], BF16)
        fold_bit = sb("fold_bit", [P, FOLD, SLOTS], I32)
        fold_base = sb("fold_base", [P, FOLD, SLOTS], I32)
        pos_iota = sb("pos_iota", [P, P])
        row_iota = sb("row_iota", [P, 1])
        ident = sb("ident", [P, P])
        upper = sb("upper", [P, 2, P])
        ones = sb("ones", [P, SPILL])
        eps_sb = sb("eps_sb", [P, 1])
        w_ext = sb("w_ext", [P, EXT])
        a_sb = weighed[:, 0:2, :].rearrange("p a (g k) -> p (a g) k", k=2 * HD)
        wa = weighed[:, 2, :].rearrange("p (h k) -> p h k", h=H)

        bad = weighed[:, 0:2, :].rearrange("p a (g t) -> p (a g) t", t=TILES)
        bad_n = sb("bad_n", [P, 1])
        flag = sb("flag", [1, 1], I32)
        row = hit[:, :, :].rearrange("p a n -> p (a n)").bitcast(F32)
        adj_row = adj_sb[:, 0, :]
        masked_row = adj_sb[:, 0, :].bitcast(F32)
        key_row = adj_sb[:, 1, :].bitcast(F32)
        blocks = weighed[:, 0:4, :]
        turned_sb = weighed[:, 4:8, :]
        acc = weighed[:, 8, :]
        dst_sb = weighed[0:H, 9, :]

        ps_spill, ps_toT, ps_xs, ps_score, ps_y, ps_wh = (
            bank(n) for n in ("ps_spill", "ps_toT", "ps_xs", "ps_score", "ps_y", "ps_wh"))
        ps_code = [bank("ps_code0"), bank("ps_code1")]
        ps_end, ps_pick = ps_spill[:, 0:2], ps_spill[:, 64:64 + SPILL + 1]
        ps_back = ps_score[:, :]
        ps_pf = ps_score[:, 128:128 + H * SPILL]

        x_in, w_in, iotas, consts, w_ready = (sem(n) for n in ("x_in", "w_in", "iotas", "consts", "w_ready"))
        adj_in = [sem("adj_in0"), sem("adj_in1")]
        early_gathered = [sem("early_gathered0"), sem("early_gathered1")]
        late_gathered = [sem("late_gathered0"), sem("late_gathered1")]
        spill_gathered = [sem("spill_gathered0"), sem("spill_gathered1")]
        stored = [sem("stored0"), sem("stored1")]
        names = ("hit_ready packed cand_done idx_ready idx_kept spill_n_ready end_ready map_ready mapT_ready maps_done "
                 "spill_idx_ready scored spread_ready back_ready neg_max_ready prob_ready pf_ready "
                 "pf_done weighted y_ready y_read var_ready rstd_ready x1_ready x1T_ready x1T_copied wh_ready "
                 "wh_copied x1_kept").split()
        S = {n: sem(n) for n in names}
        (hit_ready, packed, cand_done, idx_ready, idx_kept, spill_n_ready, end_ready, map_ready, mapT_ready, maps_done,
         spill_idx_ready, scored, spread_ready, back_ready, neg_max_ready, prob_ready, pf_ready,
         pf_done, weighted, y_ready, y_read, var_ready, rstd_ready, x1_ready, x1T_ready, x1T_copied, wh_ready,
         wh_copied, x1_kept) = (S[n] for n in names)
        T = {n: sem("second_" + n) for n in ("end_copied map_ready mapT_ready mapT_copied spread_ready back_ready e_ready "
                                             "prob_ready pf_ready weighted y_ready y_read low_ready exp_ready "
                                             "var_ready rstd_ready out_ready idx_copied").split()}
        gathered2 = [sem("second_gathered0"), sem("second_gathered1")]
        out_stored = [sem("out_stored0"), sem("out_stored1")]
        D0, D1 = ({n: sem(f"dense{layer}_{n}") for n in (
            "adj_in tile_in key_in values_in xT_ready xT_copied scored score_copied neg_max_ready prob_ready block_ready "
            "turned turned_copied summed added pass_done var_ready rstd_ready x1_ready x1T_ready x1T_copied "
            "wh_ready wh_copied stored low_ready exp_ready out_ready").split()} for layer in range(2))
        bad_ready, bad_summed, flag_ready = (sem(n) for n in ("bad_ready", "bad_summed", "flag_ready"))
        settled = sem("settled")
        dve_chain = sem("dve_chain")
        act_chain = sem("act_chain")

        def tiles_of(engine, step, first=4):
            with engine.Fori(0, (TILES - first) // 2) as q:
                for b in range(2):
                    step(q * 2 + (first + b), q + (first + b) // 2, b)

        def sparse(engine):
            engine.wait_ge(flag_ready, 1)
            return engine.value_load(flag[0:1, 0:1], min_val=0, max_val=1)

        def turns(engine, step):
            engine.sem_inc(settled, 1)
            with engine.Fori(0, GROUPS) as g:
                step(g)

        def dense_loads(sp):
            sp.dma_start(x_sb[:, :, :], ks.rearrange("(t p) d -> p t d", p=P)).then_inc(D0["values_in"], 16)
            with sp.Fori(0, TILES) as t:
                sp.wait_ge(D0["pass_done"], t + 1)
                sp.sem_inc(settled, 1)
                sp.dma_start(adj_row, adj[bass.ds(t * P, P), :]).then_inc(D0["adj_in"], 16)
                sp.dma_start(z[:, 0, :], x[bass.ds(t * P, P), :]).then_inc(D0["tile_in"], 16)
                sp.wait_ge(D0["wh_copied"], t + 2)
                sp.sem_inc(settled, 1)
                sp.dma_start(wh_dram[bass.ds(t * P, P), :], wh_sb[:, 0, 0:ROW]).then_inc(D0["stored"], 16)
                sp.dma_start(dst_dram[:, bass.ds(t * P, P)], dst_sb).then_inc(D0["stored"], 16)
                sp.dma_start(x1_dram[bass.ds(t * P, P), :], x1[:, 0, :]).then_inc(D0["stored"], 16)
                sp.wait_ge(D0["stored"], t * 48 + 48)
                sp.sem_inc(settled, 1)
            sp.wait_ge(D0["pass_done"], TILES + 1)
            sp.dma_start(x_sb[:, :, :], wh_dram[:, 0:D].rearrange("(t p) d -> p t d", p=P)).then_inc(D1["values_in"], 16)
            with sp.Fori(0, TILES) as t:
                for h in range(H):
                    sp.wait_ge(D1["pass_done"], t * H + h + 1)
                    sp.sem_inc(settled, 1)
                    if h == 0:
                        sp.dma_start(z[:, 0, :], x1_dram[bass.ds(t * P, P), :]).then_inc(D1["tile_in"], 16)
                    sp.dma_start(adj_row, adj[bass.ds(t * P, P), :]).then_inc(D1["adj_in"], 16)
                    sp.dma_start(key_row, dst_dram[h:h + 1, :].to_broadcast([P, N])).then_inc(D1["key_in"], 16)
                sp.wait_ge(D1["out_ready"], t + 2)
                sp.sem_inc(settled, 1)
                sp.dma_start(out[bass.ds(t * P, P), :], x1[:, 0, :]).then_inc(D1["stored"], 16)
                sp.wait_ge(D1["stored"], t * 16 + 16)
                sp.sem_inc(settled, 1)
            sp.wait_ge(D1["stored"], 16 * TILES)

        def dense_scalar(act):
            def turn(S, src, dst, m):
                act.wait_ge(S["turned"], m + 1)
                act.activation(blocks.rearrange("p a d -> p (a d)"), src, ACT.Copy).then_inc(S["block_ready"], 1)
                act.wait_ge(S["turned"], m + 2)
                act.activation(dst, ps_toT[:, :], ACT.Copy).then_inc(S["turned_copied"], 1)

            def exp_and_turn(S, n, base):
                act.wait_ge(S["neg_max_ready"], n + 2)
                act.activation(row, row, ACT.Exp, bias=neg_max[:, 0, :],
                               accum_out=rsum[:, 0, 0:1]).then_inc(S["prob_ready"], 1)
                act.wait_ge(S["prob_ready"], n + 2)

                def values_turn(g):
                    act.wait_ge(S["summed"], n * GROUPS + g + 1)
                    turn(S, row[:, bass.ds(g * 512, 512)], turned_sb.rearrange("p a d -> p (a d)"), n * GROUPS + g + base)

                turns(act, values_turn)

            def root(S, n):
                act.wait_ge(S["var_ready"], n + 2)
                act.activation(ln_var[:, :], mv[:, 0, 1:2], ACT.Ln, bias=eps_sb[:, :]).then_inc(act_chain, 1)
                act.wait_ge(act_chain, n + (TILES + 1 + (TILES if S is D1 else 0)))
                act.activation(rstd[:, 0, :], ln_var[:, :], ACT.Exp, scale=-0.5).then_inc(S["rstd_ready"], 1)

            act.wait_ge(D0["values_in"], 16)
            turns(act, lambda g: turn(D0, x_sb[:, bass.ds(g * 4, 4), :].rearrange("p a d -> p (a d)"),
                                      key_row[:, bass.ds(g * 512, 512)], g))
            with act.Fori(0, TILES) as t:
                act.wait_ge(D0["xT_ready"], t + 2)
                act.activation(x1T[:, :], ps_wh[:, 0:P], ACT.Copy).then_inc(D0["xT_copied"], 1)
                exp_and_turn(D0, t, GROUPS)
                root(D0, t)
                act.wait_ge(D0["x1T_ready"], t + 2)
                act.activation(x1T[:, :], ps_wh[:, 0:P], ACT.Copy).then_inc(D0["x1T_copied"], 1)
                act.wait_ge(D0["wh_ready"], t + 2)
                act.activation(src_all[:, bass.ds(t, 1), :].rearrange("p a h -> p (a h)"), ps_wh[:, ROW:EXT], ACT.Copy)
                act.activation(dst_sb, ps_xs[0:H, 0:P], ACT.Copy)
                act.activation(wh_sb[:, 0, 0:ROW], ps_wh[:, 0:ROW], ACT.Copy).then_inc(D0["wh_copied"], 1)
            with act.Fori(0, TILES) as t:
                for h in range(H):
                    exp_and_turn(D1, t * H + h, 0)
                act.wait_ge(D1["low_ready"], t + 2)
                act.activation(elu_exp[:, :], elu_low[:, :], ACT.Exp).then_inc(D1["exp_ready"], 1)
                root(D1, t)

        def dense_vector(dve, restart_chain, link, at):
            def softmax_and_sum(S, n):
                link(nc.vector.scalar_tensor_tensor(row, row, LEAK, row, ALU.mult, ALU.max))
                link(nc.vector.scalar_tensor_tensor(row, adj_row, 0.0, row, ALU.is_gt, ALU.mult))
                link(nc.vector.tensor_scalar(masked_row, adj_row, 0.0, MASKED, ALU.is_le, ALU.mult))
                link(nc.vector.tensor_tensor(row, row, masked_row, ALU.add))
                link(nc.vector.tensor_reduce(rmax[:, 0:1], row, AX, ALU.max))
                nc.vector.tensor_scalar(neg_max[:, 0, :], rmax[:, 0:1], -1.0, None, ALU.mult).then_inc(S["neg_max_ready"], 1)
                link(nc.vector.memset(acc, 0.0))
                dve.wait_ge(S["prob_ready"], n + 2)
                link(nc.vector.reciprocal(rinv[:, 0, 0:1], rsum[:, 0, 0:1]))

                def add(g):
                    dve.wait_ge(S["summed"], n * GROUPS + g + 2)
                    nc.vector.tensor_tensor(acc, acc, ps_y[:, 0:D], ALU.add).then_inc(S["added"], 1)
                    dve.wait_ge(S["added"], n * GROUPS + g + 2)

                turns(dve, add)

            def norm(S, n, done):
                link(nc.vector.bn_stats(stats[:, :], z[:, 1, :]))
                nc.vector.bn_aggr(mv[:, 0, :], stats[:, :]).then_inc(S["var_ready"], 1)
                dve.wait_ge(S["rstd_ready"], n + 2)
                nc.vector.tensor_scalar(x1[:, 0, :], z[:, 1, :], mv[:, 0, 0:1], rstd[:, 0, :], ALU.subtract,
                                        ALU.mult).then_inc(done, 1)

            with dve.Fori(0, TILES) as t:
                restart_chain()

                def copy_scores(c):
                    dve.wait_ge(D0["scored"], t * GROUPS + c + 2)
                    nc.vector.tensor_copy(row[:, bass.ds(c * 512, 512)], ps_back[:, :]).then_inc(D0["score_copied"], 1)

                turns(dve, copy_scores)
                dve.wait_ge(D0["score_copied"], t * GROUPS + GROUPS + 1)
                dve.wait_ge(D0["adj_in"], t * 16 + 16)
                softmax_and_sum(D0, t)
                dve.wait_ge(D0["tile_in"], t * 16 + 16)
                link(nc.vector.scalar_tensor_tensor(z[:, 1, :], acc, rinv[:, 0, 0:1], z[:, 0, :], ALU.mult, ALU.add))
                norm(D0, t, D0["x1_ready"])
                dve.wait_ge(D0["x1T_copied"], t + 2)
                link(nc.vector.memset(score_spill[:, :], 0.0))
                nc.vector.memset(score_spill[:, :], 0.0).then_inc(D0["pass_done"], 1)
            dve.wait_ge(D0["wh_copied"], TILES + 1)
            with dve.Fori(0, TILES) as t:
                for h in range(H):
                    restart_chain()
                    n = t * H + h
                    dve.wait_ge(D1["key_in"], n * 16 + 16)
                    dve.wait_ge(D1["adj_in"], n * 16 + 16)
                    link(nc.vector.tensor_copy(spill_n[:, :], at(src_all, t)[:, h:h + 1]))
                    link(nc.vector.tensor_scalar(row, key_row, spill_n[:, :], None, ALU.add))
                    softmax_and_sum(D1, n)
                    link(nc.vector.tensor_scalar(hn[:, h * HD:(h + 1) * HD], acc[:, h * HD:(h + 1) * HD],
                                                 rinv[:, 0, 0:1], None, ALU.mult))
                    nc.vector.memset(score_spill[:, :], 0.0).then_inc(D1["pass_done"], 1)
                restart_chain()
                nc.vector.tensor_scalar(elu_low[:, :], hn[:, :], 0.0, None, ALU.min).then_inc(D1["low_ready"], 1)
                dve.wait_ge(D1["exp_ready"], t + 2)
                link(nc.vector.scalar_tensor_tensor(hn[:, :], hn[:, :], 0.0, elu_exp[:, :], ALU.max, ALU.add))
                dve.wait_ge(D1["tile_in"], t * 16 + 16)
                link(nc.vector.scalar_tensor_tensor(z[:, 1, :], hn[:, :], -1.0, z[:, 0, :], ALU.add, ALU.add))
                norm(D1, t, D1["out_ready"])
                link(nc.vector.memset(score_spill[:, :], 0.0))

        def dense_tensor(pe):
            mm = nc.tensor.matmul

            def turn(S, m):
                pe.wait_ge(S["block_ready"], m + 2)
                pe.wait_ge(S["turned_copied"], m + 1)
                for k in range(4):
                    last = nc.tensor.transpose(ps_toT[:, k * P:(k + 1) * P], blocks[:, k, :], ident[:, :])
                last.then_inc(S["turned"], 1)

            def sum_values(S, n, base):
                def group(g):
                    turn(S, n * GROUPS + g + base)
                    pe.wait_ge(S["turned_copied"], n * GROUPS + g + (base + 1) + 1)
                    pe.wait_ge(S["added"], n * GROUPS + g + 1)
                    for k in range(4):
                        last = mm(ps_y[:, 0:D], turned_sb[:, k, :],
                                  x_sb[:, bass.ds(g * 4 + k, 1), :].rearrange("p a d -> p (a d)"),
                                  start=(k == 0), stop=(k == 3))
                    last.then_inc(S["summed"], 1)

                turns(pe, group)

            turns(pe, lambda g: turn(D0, g))
            pe.wait_ge(D0["turned_copied"], GROUPS + 1)
            with pe.Fori(0, TILES) as t:
                pe.wait_ge(D0["tile_in"], t * 16 + 16)
                pe.wait_ge(D0["wh_copied"], t + 1)
                nc.tensor.transpose(ps_wh[:, 0:P], z[:, 0, :], ident[:, :]).then_inc(D0["xT_ready"], 1)
                pe.wait_ge(D0["xT_copied"], t + 2)

                def scores(c):
                    pe.wait_ge(D0["score_copied"], t * GROUPS + c + 1)
                    mm(ps_back[:, :], x1T[:, :], key_row[:, bass.ds(c * 512, 512)], start=True,
                       stop=True).then_inc(D0["scored"], 1)

                turns(pe, scores)
                sum_values(D0, t, GROUPS)
                pe.wait_ge(D0["x1_ready"], t + 2)
                nc.tensor.transpose(ps_wh[:, 0:P], x1[:, 0, :], ident[:, :]).then_inc(D0["x1T_ready"], 1)
                pe.wait_ge(D0["x1T_copied"], t + 2)
                mm(ps_xs[0:H, 0:P], w_ext[:, D:ROW], x1T[:, :], start=True, stop=True)
                mm(ps_wh[:, 0:EXT], x1T[:, :], w_ext[:, :], start=True, stop=True).then_inc(D0["wh_ready"], 1)
            pe.wait_ge(D1["values_in"], 16)
            with pe.Fori(0, TILES) as t:
                for h in range(H):
                    sum_values(D1, t * H + h, 0)

        block = ctx.enter_context(nc.Block())

        @block.sync
        def _(sp):
            sp.dma_start(w_ext[:, 0:D], W).then_inc(w_in, 16)
            sp.dma_start(a_sb, a.to_broadcast([P, H, 2 * HD])).then_inc(w_in, 16)

            def load_adj(t, half, b):
                sp.dma_start(adj_sb[:, b, 0:N // 2], adj[bass.ds(t * P, P), 0:N // 2]).then_inc(adj_in[b], 16)
                sp.wait_ge(adj_in[b], half * 32 + 16)
                sp.sem_inc(settled, 1)
                sp.dma_start(adj_sb[:, b, N // 2:N], adj[bass.ds(t * P, P), N // 2:N]).then_inc(adj_in[b], 16)

            def store_wh(t, b):
                sp.wait_ge(wh_copied, t + 1)
                sp.dma_start(wh_dram[bass.ds(t * P, P), :], wh_sb[:, b, 0:ROW]).then_inc(stored[b], 16)

            load_adj(0, 0, 0)
            sp.dma_start(x_sb[:, :, :], x_v).then_inc(x_in, 16)
            load_adj(1, 0, 1)

            def step(t, half, b):
                sp.wait_ge(hit_ready, t - 1)
                load_adj(t, half, b)

            step(2, 1, 0)
            step(3, 1, 1)

            def both(t, half, b):
                step(t, half, b)
                store_wh(t - 6, b)

            step(4, 2, 0)
            step(5, 2, 1)
            tiles_of(sp, both, 6)
            for t in range(TILES - 6, TILES):
                store_wh(t, t % 2)

            with sp.If(sparse(sp) == 0):
                def store_out(t, half, b):
                    sp.wait_ge(T["out_ready"], t + 1)
                    sp.dma_start(out[bass.ds(t * P, P), :], x1[:, b, :]).then_inc(out_stored[b], 16)

                tiles_of(sp, store_out, 0)
                for b in range(2):
                    sp.wait_ge(out_stored[b], 16 * (TILES // 2))
            with sp.Else():
                dense_loads(sp)

        @block.gpsimd
        def _(pool):
            nc.gpsimd.iota(pos_high[:, :], [[1, POS // 256]], base=0, channel_multiplier=0,
                           allow_small_or_imprecise_dtypes=True).then_inc(iotas, 1)
            nc.gpsimd.iota(pos_low[:, :], [[1, 256]], base=0, channel_multiplier=0,
                           allow_small_or_imprecise_dtypes=True).then_inc(iotas, 1)
            nc.gpsimd.iota(fold_base[:, :, :], [[POS, FOLD], [0, SLOTS]], base=N, channel_multiplier=0,
                           allow_small_or_imprecise_dtypes=True).then_inc(iotas, 1)
            nc.gpsimd.iota(pos_iota[:, :], [[1, P]], base=0, channel_multiplier=0,
                           allow_small_or_imprecise_dtypes=True).then_inc(iotas, 1)
            nc.gpsimd.iota(row_iota[:, :], [[0, 1]], base=0, channel_multiplier=1,
                           allow_small_or_imprecise_dtypes=True).then_inc(iotas, 1)

            def gather(t, half, b):
                pool.wait_ge(idx_ready, t + 1)
                if not isinstance(t, int) or t >= 2:
                    pool.wait_ge(weighted, t - 1)
                    pool.wait_ge(scored, t - 1)
                pool.sem_inc(settled, 1)
                for s in range(PRIMARY):
                    pool.indirect_dma_start(
                        out=keys[:, b, s, 0:D], out_offset=None, in_=ks,
                        in_offset=bass.IndirectOffsetOnAxis(ap=idx[:, b, s:s + 1], axis=0)
                    ).then_inc(early_gathered[b] if s < EARLY else late_gathered[b], 16)
                pool.wait_ge(spill_idx_ready, t + 1)
                pool.sem_inc(settled, 1)
                pool.indirect_dma_start(
                    out=keys[:, b, PRIMARY, 0:D], out_offset=None, in_=ks,
                    in_offset=bass.IndirectOffsetOnAxis(ap=idx[:, b, PRIMARY:PRIMARY + 1], axis=0)
                ).then_inc(spill_gathered[b], 16)

            gather(0, 0, 0)
            gather(1, 0, 1)
            tiles_of(pool, gather, 2)

            with pool.If(sparse(pool) == 0):
                for b in range(2):
                    pool.wait_ge(stored[b], 16 * (TILES // 2))
                pool.wait_ge(y_ready, TILES)

                def gather2(t, half, b):
                    pool.wait_ge(T["idx_copied"], t + 1)
                    if not isinstance(t, int) or t >= 2:
                        pool.wait_ge(T["y_ready"], t - 1)
                    pool.sem_inc(settled, 1)
                    for s in range(PRIMARY + 1):
                        pool.indirect_dma_start(
                            out=keys[:, b, s, :], out_offset=None, in_=wh_dram,
                            in_offset=bass.IndirectOffsetOnAxis(ap=idx[:, b, s:s + 1], axis=0)).then_inc(gathered2[b], 16)

                gather2(0, 0, 0)
                gather2(1, 0, 1)
                tiles_of(pool, gather2, 2)
            with pool.Else():
                pool.wait_ge(flag_ready, 1)

        @block.scalar
        def _(act):
            act.preload_act_table_set("natural_log_exp_and_others")

            def hits(t, half, b):
                act.wait_ge(adj_in[b], half * 32 + 32)
                if not isinstance(t, int) or t >= 2:
                    act.wait_ge(packed, t - 1)
                act.activation(hit[:, b, :], adj_sb[:, b, :], ACT.Relu,
                               accum_out=edge_sum[:, bass.ds(t, 1)]).then_inc(hit_ready, 1)

            def root(t, half, b):
                act.wait_ge(var_ready, t + 1)
                act.activation(ln_var[:, :], mv[:, b, 1:2], ACT.Ln, bias=eps_sb[:, :]).then_inc(act_chain, 1)
                act.wait_ge(act_chain, t + 1)
                act.activation(rstd[:, b, :], ln_var[:, :], ACT.Exp, scale=-0.5).then_inc(rstd_ready, 1)

            def keep_x1(t, half, b):
                act.wait_ge(x1_ready, t + 1)
                act.activation(x_sb[:, bass.ds(t, 1), :].rearrange("p a d -> p (a d)"), x1[:, b, :],
                               ACT.Copy).then_inc(x1_kept, 1)
                act.wait_ge(x1T_ready, t + 1)
                act.activation(x1T[:, :], ps_wh[:, 0:P], ACT.Copy).then_inc(x1T_copied, 1)

            def keep_wh(t, half, b):
                act.wait_ge(wh_ready, t + 1)
                if not isinstance(t, int) or t >= 2:
                    act.wait_ge(stored[b], half * 16)
                act.activation(src_all[:, bass.ds(t, 1), :].rearrange("p a h -> p (a h)"), ps_wh[:, ROW:EXT], ACT.Copy)
                act.activation(wh_sb[:, b, 0:ROW], ps_wh[:, 0:ROW], ACT.Copy).then_inc(wh_copied, 1)

            def keep_idx(t, half, b):
                act.wait_ge(spill_idx_ready, t + 1)
                act.activation(idx_all[:, bass.ds(t, 1), :].rearrange("p a n -> p (a n)"), idx[:, b, :],
                               ACT.Copy).then_inc(idx_kept, 1)

            def softmax(t, half, b):
                act.wait_ge(neg_max_ready, t + 1)
                act.activation(prob[:, b, 0, :], score[:, :], ACT.Exp, bias=neg_max[:, b, :],
                               accum_out=rsum[:, b, 0:1]).then_inc(prob_ready, 1)

            def copy_map(t, half, b):
                act.wait_ge(mapT_ready, t + 1)
                if not isinstance(t, int) or t >= 2:
                    act.wait_ge(y_ready, t - 1)
                act.activation(to_row[:, b, :], ps_toT[:, 0:P], ACT.Copy).then_inc(maps_done, 1)

            def weigh(t, half, b, between=None):
                if not isinstance(t, int) or t >= 1:
                    act.wait_ge(y_ready, t)
                act.wait_ge(prob_ready, t + 1)
                for s in range(PRIMARY):
                    if s == PRIMARY // 2 and between is not None:
                        keep_wh(*between)
                    act.activation(weighed[:, s, :], keys[:, b, s, 0:D], ACT.Copy, scale=prob[:, b, 0, s:s + 1])
                act.wait_ge(pf_done, t + 1)
                act.activation(weighed[:, PRIMARY, :], keys[:, b, PRIMARY, 0:D], ACT.Copy,
                               scale=prob_spill[:, b, 0:1]).then_inc(weighted, 1)

            def step(t, half, b, lists=True, attend=True, end=True):
                if end:
                    weigh(t - 2, half - 1, b, None if isinstance(t, int) and t == 2 else (t - 3, half - 2 + b, 1 - b))
                if not isinstance(t, int) or t < TILES - 2:
                    hits(t + 2, half + 1, b)
                if lists:
                    copy_map(t, half, b)
                if end:
                    root(t - 2, half - 1, b)
                if lists:
                    keep_idx(t, half, b)
                if attend:
                    softmax(t - 1, half - 1 + b, 1 - b)
                if end:
                    keep_x1(t - 2, half - 1, b)

            act.wait_ge(consts, 1)
            hits(0, 0, 0)
            hits(1, 0, 1)
            step(0, 0, 0, attend=False, end=False)
            step(1, 0, 1, end=False)
            step(2, 1, 0)
            step(3, 1, 1)
            with act.Fori(0, (TILES - 6) // 2) as q:
                for b in range(2):
                    step(q * 2 + (4 + b), q + 2, b)
            step(TILES - 2, TILES // 2 - 1, 0)
            step(TILES - 1, TILES // 2 - 1, 1)
            step(TILES, TILES // 2, 0, lists=False)
            step(TILES + 1, TILES // 2, 1, lists=False, attend=False)
            keep_wh(TILES - 1, TILES // 2 - 1, 1)

            with act.If(sparse(act) == 0):
                def copy_idx(t, half, b):
                    if not isinstance(t, int) or t >= 2:
                        act.wait_ge(gathered2[b], half * (16 * PRIMARY + 16))
                    act.activation(idx[:, b, :], idx_all[:, bass.ds(t, 1), :].rearrange("p a n -> p (a n)"),
                                   ACT.Copy).then_inc(T["idx_copied"], 1)

                def copy_ends(t, half, b):
                    act.activation(spill_end[:, b, :], end_all[:, bass.ds(t, 1), :].rearrange("p a n -> p (a n)"), ACT.Copy).then_inc(T["end_copied"], 1)

                def copy_map2(t, half, b):
                    act.wait_ge(T["mapT_ready"], t + 1)
                    act.activation(to_row[:, b, :], ps_toT[:, 0:P], ACT.Copy).then_inc(T["mapT_copied"], 1)

                def softmax2(t, half, b):
                    act.wait_ge(T["e_ready"], t + 1)
                    act.activation(prob[:, b, :, :], e[:, :, :], ACT.Exp).then_inc(T["prob_ready"], 1)

                def finish2(t, half, b):
                    act.wait_ge(T["low_ready"], t + 1)
                    act.activation(elu_exp[:, :], elu_low[:, :], ACT.Exp).then_inc(T["exp_ready"], 1)
                    act.wait_ge(T["var_ready"], t + 1)
                    act.activation(ln_var[:, :], mv[:, b, 1:2], ACT.Ln, bias=eps_sb[:, :]).then_inc(act_chain, 1)
                    act.wait_ge(act_chain, t + (TILES + 1))
                    act.activation(rstd[:, b, :], ln_var[:, :], ACT.Exp, scale=-0.5).then_inc(T["rstd_ready"], 1)

                def step2(t, half, b, maps=True, attend=True, end=True):
                    if maps:
                        copy_idx(t, half, b)
                        if not isinstance(t, int) or t >= 2:
                            act.wait_ge(T["map_ready"], t - 1)
                        copy_ends(t, half, b)
                        copy_map2(t, half, b)
                    if attend:
                        softmax2(t - 1, half - 1 + b, 1 - b)
                    if end:
                        finish2(t - 2, half - 1, b)

                act.wait_ge(idx_kept, TILES)
                for b in range(2):
                    act.wait_ge(late_gathered[b], 16 * (PRIMARY - EARLY) * (TILES // 2))
                    act.wait_ge(early_gathered[b], 16 * EARLY * (TILES // 2))
                    act.wait_ge(spill_gathered[b], 16 * (TILES // 2))
                step2(0, 0, 0, attend=False, end=False)
                step2(1, 0, 1, end=False)
                step2(2, 1, 0)
                step2(3, 1, 1)
                tiles_of(act, step2)
                step2(TILES, TILES // 2, 0, maps=False)
                finish2(TILES - 1, TILES // 2 - 1, 1)
            with act.Else():
                dense_scalar(act)

        @block.vector
        def _(dve):
            count = [0]
            dot_written = [0] * PRIMARY

            def restart_chain():
                dve.sem_clear(dve_chain)
                count[0] = 0

            def mark(ins):
                count[0] += 1
                ins.then_inc(dve_chain, 1)

            def link(ins):
                mark(ins)
                dve.wait_ge(dve_chain, count[0])

            def at(buf, t):
                return buf[:, bass.ds(t, 1), :].rearrange("p a n -> p (a n)")

            def spread_over(ap, n, d):
                return ap.rearrange("p (a d) -> p a d", a=1).to_broadcast([P, n, d])

            def each(ap, n, d):
                return ap.rearrange("p (n a) -> p n a", a=1).to_broadcast([P, n, d])

            nc.vector.memset(ones[:, :], 1.0)
            nc.vector.memset(eps_sb[:, :], EPS)
            dve.wait_ge(iotas, 5)
            link(nc.vector.tensor_scalar(ident[:, :], pos_iota[:, :], row_iota[:, 0:1], None, ALU.is_equal))
            link(nc.vector.tensor_scalar(upper[:, 0, :], pos_iota[:, :], row_iota[:, 0:1], None, ALU.is_gt))
            link(nc.vector.tensor_scalar(upper[:, 1, :], pos_iota[:, :], row_iota[:, 0:1], None, ALU.is_ge))
            for k in range(FOLD):
                nc.vector.tensor_scalar(scaled_id[:, k, :], ident[:, :], float(POS * 2 ** k), None, ALU.mult)
                nc.vector.memset(fold_bit[:, k, :], POS * 2 ** k)
            nc.vector.tensor_scalar(scaled_id[:, FOLD, :], ident[:, :], 256.0, None, ALU.mult)
            nc.vector.tensor_scalar(scaled_id[:, FOLD + 1, :], ident[:, :], 1.0, None, ALU.mult).then_inc(consts, 1)
            dve.wait_ge(w_in, 32)
            for k, lo in ((0, HD), (1, 0)):
                link(nc.vector.tensor_tensor(wa, w_ext[:, 0:D].rearrange("p (h k) -> p h k", h=H),
                                             a_sb[:, :, lo:lo + HD], ALU.mult))
                link(nc.vector.tensor_reduce(w_ext[:, D + k * H:D + (k + 1) * H], wa, AX, ALU.add))
            nc.vector.memset(score_spill[:, :], 0.0).then_inc(w_ready, 1)

            def candidates(t, half, b):
                dve.wait_ge(packed, t + 1)
                dve.sem_inc(settled, 1)
                for c in range(NCH):
                    at_c = c * CHUNK % 512
                    last = nc.vector.max(cand[:, 8 * c:8 * c + 8], ps_code[c * CHUNK // 512][:, at_c:at_c + CHUNK])
                last.then_inc(cand_done, 1)

            def largest(dst, src, between=None):
                for r in range(0, SLOTS, 8):
                    for k, step in enumerate((lambda: nc.vector.max(dst[:, r:r + 8], src),
                                              lambda: nc.vector.match_replace(src, dst[:, r:r + 8], src, 0.0))):
                        if r + 8 * k < SLOTS:
                            count[0] += 1
                            written = count[0]
                            step().then_inc(dve_chain, 1)
                            if between is not None:
                                between(r // 4 + k)
                            dve.wait_ge(dve_chain, written)

            def sort_codes(t, half, b, prev=None):
                candidates(t, half, b)
                dve.wait_ge(cand_done, t + 1)
                dve.sem_inc(settled, 1)
                if prev is None:
                    largest(codes[:, :], cand[:, :])
                else:
                    late_gathers(*prev)
                    largest(codes[:, :], cand[:, :],
                            lambda i: dot(EARLY + i - 1, prev[0], prev[2]) if 1 <= i < PRIMARY - EARLY - 2 else None)

            def lists(t, half, b, prev=None, last=None):
                link(nc.vector.tensor_copy(code_int[:, :], codes[:, :]))
                by_fold = spread_over(code_int[:, :], FOLD, SLOTS)
                mark(nc.vector.scalar_tensor_tensor(grid_cols[:, :, :], by_fold, POS - 1, fold_base[:, :, :],
                                                    ALU.bitwise_and, ALU.bitwise_or))
                link(nc.vector.tensor_tensor(grid_bits[:, :, :], fold_bit[:, :, :], by_fold, ALU.bitwise_and))
                flat = grid[:, :, :].rearrange("p k s -> p (k s)")
                link(nc.vector.scalar_tensor_tensor(flat, grid_bits[:, :, :].rearrange("p k s -> p (k s)"), 0.0,
                                                    grid_cols[:, :, :].rearrange("p k s -> p (k s)"),
                                                    ALU.is_gt, ALU.mult))
                if last is not None:
                    spill_prob(*last)
                if prev is None:
                    largest(cols[:, b, :], flat)
                else:
                    early_gathers(*prev)
                    largest(cols[:, b, :], flat, lambda s: dot(s, prev[0], prev[2]))
                nc.vector.scalar_tensor_tensor(spill_gt[:, :], cols[:, b, PRIMARY:SLOTS], 0.0, ones[:, :], ALU.is_gt,
                                               ALU.mult, accum_out=spill_n[:, :]).then_inc(spill_n_ready, 1)
                if not isinstance(t, int) or t >= 2:
                    dve.wait_ge(idx_kept, t - 1)
                    dve.wait_ge(early_gathered[b], half * (16 * EARLY))
                    dve.wait_ge(late_gathered[b], half * (16 * (PRIMARY - EARLY)))
                    dve.wait_ge(spill_gathered[b], half * 16)
                nc.vector.tensor_scalar(idx[:, b, 0:PRIMARY], cols[:, b, 0:PRIMARY], float(-N), 0.0, ALU.add,
                                        ALU.max).then_inc(idx_ready, 1)
                link(nc.vector.tensor_scalar(at(neg_all, t), cols[:, b, :], 0.0, MASKED, ALU.is_le, ALU.mult))

            def spill_map(t, half, b):
                dve.wait_ge(end_ready, t + 1)
                mark(nc.vector.tensor_copy(spill_end[:, b, :], ps_end[:, 0:2]))
                link(nc.vector.tensor_copy(at(end_all, t), ps_end[:, 0:2]))
                make_map(b).then_inc(map_ready, 1)

            def make_map(b):
                link(nc.vector.tensor_scalar(below_end[:, :], pos_iota[:, :], spill_end[:, b, 1:2], None, ALU.is_lt))
                return nc.vector.scalar_tensor_tensor(to_spill[:, b, :], pos_iota[:, :], spill_end[:, b, 0:1],
                                                      below_end[:, :], ALU.is_ge, ALU.mult)

            def spill_idx(t, half, b, between):
                dve.wait_ge(mapT_ready, t + 1)
                mark(nc.vector.scalar_tensor_tensor(slot_of[:, :], ps_pick[:, SPILL:SPILL + 1], -1.0,
                                                    row_iota[:, :], ALU.mult, ALU.add))
                written = count[0]
                between(PRIMARY - 2)
                dve.wait_ge(dve_chain, written)
                mark(nc.vector.scalar_tensor_tensor(picked[:, 0:SPILL], pos_iota[:, 0:SPILL], slot_of[:, 0:1],
                                                    ps_pick[:, 0:SPILL], ALU.is_equal, ALU.mult,
                                                    accum_out=col_spill[:, :]))
                written = count[0]
                between(PRIMARY - 1)
                mark(nc.vector.tensor_scalar(at(slot_all, t), pos_iota[:, 0:SPILL], slot_of[:, 0:1], None, ALU.is_equal))
                dve.wait_ge(dve_chain, written)
                nc.vector.tensor_scalar(idx[:, b, PRIMARY:PRIMARY + 1], col_spill[:, :], float(-N), 0.0, ALU.add,
                                        ALU.max).then_inc(spill_idx_ready, 1)

            def early_gathers(t, half, b):
                dve.wait_ge(early_gathered[b], half * (16 * EARLY) + 16 * EARLY)
                dve.sem_inc(settled, 1)

            def late_gathers(t, half, b):
                dve.wait_ge(late_gathered[b], half * (16 * (PRIMARY - EARLY)) + 16 * (PRIMARY - EARLY))
                dve.sem_inc(settled, 1)

            def dot(s, t, b):
                if s >= 4:
                    dve.wait_ge(dve_chain, dot_written[s - 4])
                nc.vector.scalar_tensor_tensor(prod[:, s % 4, :], keys[:, b, s, 0:D], 1.0, at(x_sb, t), ALU.mult,
                                               ALU.mult, accum_out=score[:, s:s + 1]).then_inc(dve_chain, 1)
                count[0] += 1
                dot_written[s] = count[0]

            def spill_dots(t, half, b):
                dve.wait_ge(dve_chain, count[0])
                dve.wait_ge(spill_gathered[b], half * 16 + 16)
                link(nc.vector.scalar_tensor_tensor(prod[:, 0, :], keys[:, b, PRIMARY, 0:D], 1.0,
                                                    ps_xs[:, b * D:(b + 1) * D],
                                                    ALU.mult, ALU.mult, accum_out=score_spill[:, :]))
                nc.vector.tensor_scalar(spread[:, 0:SPILL], at(slot_all, t), score_spill[:, 0:1], None,
                                        ALU.mult).then_inc(scored, 1)

            def mask_primary(t):
                mark(nc.vector.tensor_tensor(score[:, 0:PRIMARY], score[:, 0:PRIMARY], at(neg_all, t)[:, 0:PRIMARY], ALU.add))

            def maxima(t, half, b):
                dve.wait_ge(back_ready, t + 1)
                link(nc.vector.tensor_tensor(score[:, PRIMARY:SLOTS], ps_back[:, 0:SPILL], at(neg_all, t)[:, PRIMARY:SLOTS],
                                             ALU.add))
                link(nc.vector.scalar_tensor_tensor(score[:, :], score[:, :], LEAK, score[:, :], ALU.mult, ALU.max))
                link(nc.vector.tensor_reduce(rmax[:, 0:1], score[:, :], AX, ALU.max))
                restart_chain()
                nc.vector.tensor_scalar(neg_max[:, b, :], rmax[:, 0:1], -1.0, None, ALU.mult).then_inc(neg_max_ready, 1)

            def spill_prob(t, half, b):
                dve.wait_ge(pf_ready, t + 1)
                mark(nc.vector.reciprocal(rinv[:, b, 0:1], rsum[:, b, 0:1]))
                nc.vector.scalar_tensor_tensor(picked[:, 0:SPILL], at(slot_all, t), 1.0, ps_pf[:, 0:SPILL],
                                               ALU.mult, ALU.mult, accum_out=prob_spill[:, b, 0:1]).then_inc(pf_done, 1)

            def norm_stats(zb, b):
                link(nc.vector.bn_stats(stats[:, :], zb))
                return nc.vector.bn_aggr(mv[:, b, :], stats[:, :])

            def norm_a(t, half, b):
                dve.wait_ge(y_ready, t + 1)
                link(nc.vector.scalar_tensor_tensor(z[:, b, :], ps_y[:, 0:D], rinv[:, b, 0:1], at(x_sb, t),
                                                    ALU.mult, ALU.add))
                norm_stats(z[:, b, :], b).then_inc(var_ready, 1)

            def norm_b(t, half, b):
                dve.wait_ge(rstd_ready, t + 1)
                if not isinstance(t, int) or t >= 2:
                    dve.wait_ge(x1_kept, t - 1)
                nc.vector.tensor_scalar(x1[:, b, :], z[:, b, :], mv[:, b, 0:1], rstd[:, b, :], ALU.subtract,
                                        ALU.mult).then_inc(x1_ready, 1)

            def step(t, half, b, lst=True, attend=True, end=True):
                if not attend:
                    restart_chain()
                prev, last = (t - 1, half - 1 + b, 1 - b), (t - 2, half - 1, b)
                if lst:
                    lists(t, half, b, prev if attend else None, last if end else None)
                elif attend:
                    spill_prob(*last)
                    early_gathers(*prev)
                    for s in range(EARLY):
                        dot(s, t - 1, 1 - b)
                elif end:
                    spill_prob(*last)
                more = not isinstance(t, int) or t < TILES - 1
                if more:
                    sort_codes(t + 1, half + b, 1 - b, prev if attend else None)
                elif attend:
                    late_gathers(*prev)
                    for s in range(EARLY, PRIMARY - 3):
                        dot(s, t - 1, 1 - b)
                if lst:
                    spill_map(t, half, b)
                if attend:
                    dot(PRIMARY - 3, t - 1, 1 - b)
                    if not lst:
                        dot(PRIMARY - 2, t - 1, 1 - b)
                        dot(PRIMARY - 1, t - 1, 1 - b)
                if end:
                    norm_a(*last)
                if lst:
                    spill_idx(t, half, b, (lambda s: dot(s, t - 1, 1 - b)) if attend else (lambda s: None))
                if attend:
                    spill_dots(*prev)
                    mask_primary(t - 1)
                if end:
                    norm_b(*last)
                if attend:
                    maxima(*prev)
                if not attend:
                    link(nc.vector.memset(score_spill[:, :], 0.0))

            restart_chain()
            sort_codes(0, 0, 0)
            link(nc.vector.memset(score_spill[:, :], 0.0))
            step(0, 0, 0, attend=False, end=False)
            restart_chain()
            dve.wait_ge(x_in, 16)
            step(1, 0, 1, end=False)
            step(2, 1, 0)
            step(3, 1, 1)
            with dve.Fori(0, (TILES - 6) // 2) as q:
                for b in range(2):
                    step(q * 2 + (4 + b), q + 2, b)
            step(TILES - 2, TILES // 2 - 1, 0)
            step(TILES - 1, TILES // 2 - 1, 1)
            step(TILES, TILES // 2, 0, lst=False)
            step(TILES + 1, TILES // 2, 1, lst=False, attend=False)

            restart_chain()
            link(nc.vector.tensor_scalar(bad[:, 0, :], neg_all[:, :, 0], -1.0, None, ALU.is_lt))
            link(nc.vector.tensor_scalar(bad[:, 1, :], end_all[:, :, 1], float(P), None, ALU.is_gt))
            link(nc.vector.tensor_scalar(masked_row[:, 0:TILES * SLOTS], neg_all[:, :, :].rearrange("p t s -> p (t s)"),
                                         -1.0, None, ALU.is_gt))
            link(nc.vector.tensor_reduce(bad[:, 3, :], masked_row[:, 0:TILES * SLOTS].rearrange(
                "p (t s) -> p t s", s=SLOTS), AX, ALU.add))
            link(nc.vector.tensor_tensor(bad[:, 2, :], bad[:, 3, :], edge_sum[:, :], ALU.not_equal))
            link(nc.vector.tensor_reduce(bad_n[:, :], bad[:, 0:3, :].rearrange("p k t -> p (k t)"), AX, ALU.add))
            nc.vector.memset(score_spill[:, :], 0.0).then_inc(bad_ready, 1)
            for S in (D0, D1):
                for name in S:
                    if not name.endswith("_in") and name != "stored":
                        dve.sem_inc(S[name], 1)
            dve.wait_ge(bad_summed, 1)
            nc.vector.tensor_scalar(flag[:, :], ps_end[0:1, 0:1], 1.0, None, ALU.min).then_inc(flag_ready, 1)

            with dve.If(sparse(dve) == 0):
                def maps2(t, half, b):
                    dve.wait_ge(T["end_copied"], t + 1)
                    make_map(b).then_inc(T["map_ready"], 1)

                def scores2a(t, half, b):
                    dve.wait_ge(gathered2[b], half * (16 * PRIMARY + 16) + (16 * PRIMARY + 16))
                    nc.vector.tensor_tensor(
                        spread[:, :].rearrange("p (h s) -> p h s", h=H), spread_over(at(slot_all, t), H, SPILL),
                        each(keys[:, b, PRIMARY, D:ROW], H, SPILL), ALU.mult).then_inc(T["spread_ready"], 1)
                    link(nc.vector.tensor_tensor(e[:, :, 0:PRIMARY],
                                                 keys[:, b, 0:PRIMARY, D:ROW].rearrange("p s h -> p h s"),
                                                 each(at(src_all, t), H, PRIMARY), ALU.add))

                def scores2b(t, half, b):
                    dve.wait_ge(T["back_ready"], t + 1)
                    link(nc.vector.tensor_tensor(e[:, :, PRIMARY:SLOTS],
                                                 ps_back[:, 0:H * SPILL].rearrange("p (h s) -> p h s", h=H),
                                                 each(at(src_all, t), H, SPILL), ALU.add))
                    link(nc.vector.tensor_tensor(e[:, :, :], e[:, :, :], spread_over(at(neg_all, t), H, SLOTS), ALU.add))
                    flat = e[:, :, :].rearrange("p h s -> p (h s)")
                    link(nc.vector.scalar_tensor_tensor(flat, flat, LEAK, flat, ALU.mult, ALU.max))
                    link(nc.vector.tensor_reduce(rmax[:, :], e[:, :, :], AX, ALU.max))
                    nc.vector.tensor_tensor(e[:, :, :], e[:, :, :], each(rmax[:, :], H, SLOTS),
                                            ALU.subtract).then_inc(T["e_ready"], 1)

                def weigh2(t, half, b):
                    dve.wait_ge(T["prob_ready"], t + 1)
                    by_head = keys[:, b, 0:PRIMARY, 0:D].rearrange("p s (h k) -> p s h k", h=H)
                    nc.vector.tensor_tensor(
                        by_head, by_head,
                        prob[:, b, :, 0:PRIMARY].rearrange("p h (s a) -> p s h a", a=1).to_broadcast([P, PRIMARY, H, HD]),
                        ALU.mult)
                    link(nc.vector.tensor_reduce(rsum[:, b, :], prob[:, b, :, :], AX, ALU.add))
                    link(nc.vector.reciprocal(rinv[:, b, :], rsum[:, b, :]))
                    dve.wait_ge(T["pf_ready"], t + 1)
                    link(nc.vector.tensor_tensor(picked[:, :].rearrange("p (h s) -> p h s", h=H),
                                                 ps_pf[:, 0:H * SPILL].rearrange("p (h s) -> p h s", h=H),
                                                 spread_over(at(slot_all, t), H, SPILL), ALU.mult))
                    link(nc.vector.tensor_reduce(prob_spill[:, b, :], picked[:, :].rearrange("p (h s) -> p h s", h=H),
                                                 AX, ALU.add))
                    spill = keys[:, b, PRIMARY, 0:D].rearrange("p (h k) -> p h k", h=H)
                    nc.vector.tensor_tensor(spill, spill, each(prob_spill[:, b, :], H, HD),
                                            ALU.mult).then_inc(T["weighted"], 1)

                def norm2_a(t, half, b):
                    dve.wait_ge(T["y_ready"], t + 1)
                    link(nc.vector.tensor_tensor(hn[:, :].rearrange("p (h k) -> p h k", h=H),
                                                 ps_y[:, 0:D].rearrange("p (h k) -> p h k", h=H),
                                                 each(rinv[:, b, :], H, HD), ALU.mult))
                    nc.vector.tensor_scalar(elu_low[:, :], hn[:, :], 0.0, None, ALU.min).then_inc(T["low_ready"], 1)

                def norm2_b(t, half, b):
                    dve.wait_ge(T["exp_ready"], t + 1)
                    link(nc.vector.scalar_tensor_tensor(hn[:, :], hn[:, :], 0.0, elu_exp[:, :], ALU.max, ALU.add))
                    link(nc.vector.scalar_tensor_tensor(z[:, b, :], hn[:, :], -1.0, at(x_sb, t), ALU.add, ALU.add))
                    norm_stats(z[:, b, :], b).then_inc(T["var_ready"], 1)
                    dve.wait_ge(T["rstd_ready"], t + 1)
                    if not isinstance(t, int) or t >= 2:
                        dve.wait_ge(out_stored[b], half * 16)
                    nc.vector.tensor_scalar(x1[:, b, :], z[:, b, :], mv[:, b, 0:1], rstd[:, b, :], ALU.subtract,
                                            ALU.mult).then_inc(T["out_ready"], 1)

                def step2(t, half, b, maps=True, attend=True, end=True):
                    restart_chain()
                    prev = (t - 1, half - 1 + b, 1 - b)
                    if maps:
                        maps2(t, half, b)
                    if attend:
                        scores2a(*prev)
                    if end:
                        norm2_a(t - 2, half - 1, b)
                    if attend:
                        scores2b(*prev)
                    if end:
                        norm2_b(t - 2, half - 1, b)
                    if attend:
                        weigh2(*prev)
                    link(nc.vector.memset(score_spill[:, :], 0.0))

                dve.wait_ge(x1_kept, TILES)
                dve.wait_ge(wh_copied, TILES)
                step2(0, 0, 0, attend=False, end=False)
                step2(1, 0, 1, end=False)
                step2(2, 1, 0)
                step2(3, 1, 1)
                tiles_of(dve, step2)
                step2(TILES, TILES // 2, 0, maps=False)
                restart_chain()
                norm2_a(TILES - 1, TILES // 2 - 1, 1)
                norm2_b(TILES - 1, TILES // 2 - 1, 1)
            with dve.Else():
                dense_vector(dve, restart_chain, link, at)

        @block.tensor
        def _(pe):
            mm = nc.tensor.matmul

            def pack(t, half, b, halves):
                if 0 in halves:
                    pe.wait_ge(hit_ready, t + 1)
                    if not isinstance(t, int) or t >= 1:
                        pe.wait_ge(cand_done, t)
                for c in halves:
                    for k in range(FOLD):
                        lo = k * POS + c * 512
                        mm(ps_code[c][:, :], scaled_id[:, k, :], hit[:, b, lo:lo + 512], start=(k == 0), stop=False)
                    mm(ps_code[c][:, :], scaled_id[:, FOLD, :], 
                       pos_high[:, 2 * c:2 * c + 2].rearrange("p (n a) -> p n a", a=1).to_broadcast([P, 2, 256]),
                       start=False, stop=False)
                    last = mm(ps_code[c][:, :], scaled_id[:, FOLD + 1, :],
                              pos_low[:, :].rearrange("p (a n) -> p a n", a=1).to_broadcast([P, 2, 256]),
                              start=False, stop=True)
                if 1 in halves:
                    last.then_inc(packed, 1)

            def finish(t, half, b):
                pe.wait_ge(x1_ready, t + 1)
                if not isinstance(t, int) or t >= 1:
                    pe.wait_ge(wh_copied, t)
                nc.tensor.transpose(ps_wh[:, 0:P], x1[:, b, :], ident[:, :]).then_inc(x1T_ready, 1)
                pe.wait_ge(x1T_copied, t + 1)
                mm(ps_wh[:, 0:EXT], x1T[:, :], w_ext[:, :], start=True, stop=True).then_inc(wh_ready, 1)

            def back(t, half, b):
                pe.wait_ge(scored, t + 1)
                pe.wait_ge(maps_done, t + 1)
                mm(ps_back[:, 0:SPILL], to_row[:, b, :], spread[:, 0:SPILL], start=True, stop=True).then_inc(back_ready, 1)

            def ends(t, half, b):
                pe.wait_ge(spill_n_ready, t + 1)
                mm(ps_end[:, 0:1], upper[:, 0, :], spill_n[:, :], start=True, stop=True)
                mm(ps_end[:, 1:2], upper[:, 1, :], spill_n[:, :], start=True, stop=True).then_inc(end_ready, 1)

            def maps(t, half, b):
                pe.wait_ge(map_ready, t + 1)
                mm(ps_pick[:, 0:SPILL], to_spill[:, b, :], cols[:, b, PRIMARY:SLOTS], start=True, stop=True)
                mm(ps_pick[:, SPILL:SPILL + 1], to_spill[:, b, :], spill_end[:, b, 0:1], start=True, stop=True)
                if not isinstance(t, int) or t >= 1:
                    pe.wait_ge(maps_done, t)
                mm(ps_xs[:, b * D:(b + 1) * D], to_spill[:, b, :], x_sb[:, bass.ds(t, 1), :].rearrange("p a d -> p (a d)"),
                   start=True, stop=True)
                nc.tensor.transpose(ps_toT[:, 0:P], to_spill[:, b, :], ident[:, :]).then_inc(mapT_ready, 1)

            def probs(t, half, b):
                pe.wait_ge(prob_ready, t + 1)
                mm(ps_pf[:, 0:SPILL], to_spill[:, b, :], prob[:, b, 0, PRIMARY:SLOTS], start=True,
                   stop=True).then_inc(pf_ready, 1)

            def sum_rows(rows, b, done):
                for s in range(PRIMARY):
                    mm(ps_y[:, 0:D], ident[:, :], rows[:, s, 0:D], start=(s == 0), stop=False)
                mm(ps_y[:, 0:D], to_row[:, b, :], rows[:, PRIMARY, 0:D], start=False, stop=True).then_inc(done, 1)

            def weighted_sum(t, half, b):
                pe.wait_ge(weighted, t + 1)
                if not isinstance(t, int) or t >= 1:
                    pe.wait_ge(var_ready, t)
                sum_rows(weighed, b, y_ready)

            def step(t, half, b, lst=True, attend=True, end=True):
                prev, last = (t - 1, half - 1 + b, 1 - b), (t - 2, half - 1, b)
                more = not isinstance(t, int) or t < TILES - 2
                if lst:
                    ends(t, half, b)
                if end:
                    weighted_sum(*last)
                if lst:
                    maps(t, half, b)
                if more:
                    pack(t + 2, half + 1, b, (0,))
                if attend:
                    back(*prev)
                if more:
                    pack(t + 2, half + 1, b, (1,))
                if attend:
                    probs(*prev)
                if end:
                    finish(*last)

            pe.wait_ge(consts, 1)
            pe.wait_ge(w_ready, 1)
            pack(0, 0, 0, (0, 1))
            pack(1, 0, 1, (0, 1))
            pe.wait_ge(x_in, 16)
            step(0, 0, 0, attend=False, end=False)
            step(1, 0, 1, end=False)
            step(2, 1, 0)
            step(3, 1, 1)
            with pe.Fori(0, (TILES - 6) // 2) as q:
                for b in range(2):
                    step(q * 2 + (4 + b), q + 2, b)
            step(TILES - 2, TILES // 2 - 1, 0)
            step(TILES - 1, TILES // 2 - 1, 1)
            step(TILES, TILES // 2, 0, lst=False)
            step(TILES + 1, TILES // 2, 1, lst=False, attend=False)

            pe.wait_ge(bad_ready, 1)
            mm(ps_end[0:1, 0:1], bad_n[:, :], ones[:, 0:1], start=True, stop=True).then_inc(bad_summed, 1)

            with pe.If(sparse(pe) == 0):
                def maps2(t, half, b):
                    pe.wait_ge(T["map_ready"], t + 1)
                    if not isinstance(t, int) or t >= 1:
                        pe.wait_ge(T["mapT_copied"], t)
                    nc.tensor.transpose(ps_toT[:, 0:P], to_spill[:, b, :], ident[:, :]).then_inc(T["mapT_ready"], 1)

                def back2(t, half, b):
                    pe.wait_ge(T["spread_ready"], t + 1)
                    pe.wait_ge(T["mapT_copied"], t + 1)
                    mm(ps_back[:, 0:H * SPILL], to_row[:, b, :], spread[:, :], start=True, stop=True).then_inc(T["back_ready"], 1)

                def probs2(t, half, b):
                    pe.wait_ge(T["prob_ready"], t + 1)
                    mm(ps_pf[:, 0:H * SPILL], to_spill[:, b, :], prob[:, b, :, PRIMARY:SLOTS], start=True,
                       stop=True).then_inc(T["pf_ready"], 1)

                def step2(t, half, b, maps=True, attend=True, end=True):
                    prev = (t - 1, half - 1 + b, 1 - b)
                    if maps:
                        maps2(t, half, b)
                    if attend:
                        back2(*prev)
                        probs2(*prev)
                        pe.wait_ge(T["weighted"], prev[0] + 1)
                        if not isinstance(t, int) or t >= 2:
                            pe.wait_ge(T["low_ready"], t - 1)
                        sum_rows(keys[:, 1 - b, :, :], 1 - b, T["y_ready"])

                step2(0, 0, 0, attend=False)
                step2(1, 0, 1)
                step2(2, 1, 0)
                step2(3, 1, 1)
                tiles_of(pe, step2)
                step2(TILES, TILES // 2, 0, maps=False)
            with pe.Else():
                dense_tensor(pe)

_INS = ["x", "adj", "L0_gnn_ks", "L1_gnn_W", "L1_gnn_a"]


def kernel(**inputs):
    import numpy as np
    import concourse.bacc as bacc
    from concourse.bass_utils import run_bass_kernel_spmd as run

    nc = bacc.Bacc("TRN2", target_bir_lowering=False, num_devices=1)
    arrays, args = {}, []
    for name in _INS:
        v = np.ascontiguousarray(inputs[name])
        arrays[f"in_{name}_dram"] = v
        args.append(nc.dram_tensor(f"in_{name}_dram", v.shape, mybir.dt.from_np(v.dtype), kind="ExternalInput").ap())
    out = nc.dram_tensor("out_dram", inputs["x"].shape, F32, kind="ExternalOutput").ap()
    adj_resnorm_kernel(nc, *args, out)
    return run(nc, [arrays], core_ids=[0]).results[0]["out_dram"]
```

```python
from contextlib import ExitStack

import concourse.bass as bass
from concourse import mybir

ALU = mybir.AluOpType
ACT = mybir.ActivationFunctionType
F32 = mybir.dt.float32
BF16 = mybir.dt.bfloat16
I32 = mybir.dt.int32
U32 = mybir.dt.uint32
AX = mybir.AxisListType.X

P = 128
PRIMARY = 17
EARLY = 7
SLOTS = 40
SPILL = SLOTS - PRIMARY
PART = PRIMARY // 2
BLOCKS = 2
GATHERS = PRIMARY + BLOCKS
FOLD = 8
MULTI = 8
EXPONENT = 0x7F800000
CHUNK = 64
MASKED = -9.0e15
LEAK = 0.2
EPS = 1e-5


def adj_resnorm_kernel(nc, x, adj, ks, W, a, out):
    N, D = x.shape
    H, HD = a.shape[1], a.shape[2] // 2
    TILES = N // P
    POS = N // FOLD
    NCH = POS // CHUNK
    ROW = D + H
    EXT = D + 2 * H

    wh_dram = nc.dram_tensor("wh_rows", (N, ROW), F32, kind="Internal").ap()
    x1_dram = nc.dram_tensor("x1_rows", (N, D), F32, kind="Internal").ap()
    dst_dram = nc.dram_tensor("dst_rows", (H, N), F32, kind="Internal").ap()
    GROUPS = N // 512
    x_v = x.rearrange("(t p) d -> p t d", p=P)

    with ExitStack() as ctx:
        def sb(name, shape, dt=F32):
            return ctx.enter_context(nc.sbuf_tensor(name, shape, dt))

        def bank(name):
            return ctx.enter_context(nc.psum_tensor(name, [P, 512], F32))

        def sem(name):
            return ctx.enter_context(nc.semaphore(name))

        adj_sb = sb("adj_sb", [P, 2, N], I32)
        hit = sb("hit", [P, 2, N], BF16)
        keys = sb("keys", [P, 2, GATHERS, ROW])
        weighed = sb("weighed", [P, GATHERS, D])
        prod = sb("prod", [P, 4, D])
        cand = sb("cand", [P, NCH * 8])
        codes = sb("codes", [P, SLOTS])
        code_int = sb("code_int", [P, SLOTS], I32)
        code_pos = sb("code_pos", [P, SLOTS], I32)
        top_bit = sb("top_bit", [P, SLOTS], I32)
        top_k = sb("top_k", [P, SLOTS], I32)
        top_base = sb("top_base", [P, SLOTS])
        top_col = sb("top_col", [P, SLOTS])
        rest = sb("rest", [P, SLOTS])
        multi = sb("multi", [P, MULTI])
        multi_int = sb("multi_int", [P, MULTI], I32)
        grid_bits = sb("grid_bits", [P, FOLD, MULTI], I32)
        grid_cols = sb("grid_cols", [P, FOLD, MULTI], I32)
        found = sb("found", [P, SLOTS + FOLD * MULTI])
        cols = sb("cols", [P, 2, SLOTS + 2])
        spill_end = cols[:, :, SLOTS:SLOTS + 2]
        idx = sb("idx", [P, 2, GATHERS], U32)
        spill_n = sb("spill_n", [P, 1])
        spill_gt = sb("spill_gt", [P, SPILL])
        below_end = sb("below_end", [P, BLOCKS * P])
        to_spill = sb("to_spill", [P, 2, BLOCKS * P])
        to_row = sb("to_row", [P, 2, BLOCKS * P])
        slot_hot = sb("slot_hot", [P, 2, BLOCKS, SPILL])
        picked = sb("picked", [P, BLOCKS, H * SPILL])
        col_spill = sb("col_spill", [P, BLOCKS])
        spread = sb("spread", [P, BLOCKS, H * SPILL])
        score_spill = sb("score_spill", [P, BLOCKS])
        score = sb("score", [P, SLOTS])
        e = sb("e", [P, H, SLOTS])
        prob = sb("prob", [P, 2, H, SLOTS])
        prob_spill = sb("prob_spill", [P, 2, BLOCKS, H])
        rmax = sb("rmax", [P, H])
        neg_max = sb("neg_max", [P, 2, 1])
        rsum = sb("rsum", [P, 2, H])
        rinv = sb("rinv", [P, 2, H])
        z = sb("z", [P, 2, D])
        elu_low = sb("elu_low", [P, D])
        elu_exp = sb("elu_exp", [P, D])
        hn = sb("hn", [P, D])
        stats = sb("stats", [P, 6])
        mv = sb("mv", [P, 2, 2])
        ln_var = sb("ln_var", [P, 1])
        rstd = sb("rstd", [P, 2, 1])
        x1 = sb("x1", [P, 2, D])
        x1T = sb("x1T", [P, P])
        wh_sb = sb("wh_sb", [P, 2, EXT])
        x_sb = sb("x_sb", [P, TILES, D])
        neg_all = sb("neg_all", [P, TILES, SLOTS])
        idx_all = sb("idx_all", [P, TILES, GATHERS], U32)
        slot_all = sb("slot_all", [P, TILES, BLOCKS])
        end_all = sb("end_all", [P, TILES, 2])
        src_all = sb("src_all", [P, TILES, H])
        edge_sum = sb("edge_sum", [P, TILES])
        pos_high = sb("pos_high", [P, POS // 256], BF16)
        pos_low = sb("pos_low", [P, 256], BF16)
        scaled_id = sb("scaled_id", [P, FOLD + 2, P], BF16)
        fold_bit = sb("fold_bit", [P, FOLD, MULTI], I32)
        fold_base = sb("fold_base", [P, FOLD, MULTI], I32)
        pos_iota = sb("pos_iota", [P, BLOCKS * P])
        row_iota = sb("row_iota", [P, BLOCKS])
        ident = sb("ident", [P, P])
        upper = sb("upper", [P, 2, P])
        ones = sb("ones", [P, SPILL])
        eps_sb = sb("eps_sb", [P, 1])
        w_ext = sb("w_ext", [P, EXT])
        a_sb = weighed[:, 0:2, :].rearrange("p a (g k) -> p (a g) k", k=2 * HD)
        wa = weighed[:, 2, :].rearrange("p (h k) -> p h k", h=H)

        bad = weighed[:, 0:2, :].rearrange("p a (g t) -> p (a g) t", t=TILES)
        bad_n = sb("bad_n", [P, 1])
        flag = sb("flag", [1, 1], I32)
        row = hit[:, :, :].rearrange("p a n -> p (a n)").bitcast(F32)
        adj_row = adj_sb[:, 0, :]
        masked_row = adj_sb[:, 0, :].bitcast(F32)
        key_row = adj_sb[:, 1, :].bitcast(F32)
        blocks = weighed[:, 0:4, :]
        turned_sb = weighed[:, 4:8, :]
        acc = weighed[:, 8, :]
        dst_sb = weighed[0:H, 9, :]

        ps_spill, ps_toT, ps_xs, ps_score, ps_y, ps_wh = (
            bank(n) for n in ("ps_spill", "ps_toT", "ps_xs", "ps_score", "ps_y", "ps_wh"))
        ps_code = [bank("ps_code0"), bank("ps_code1")]
        ps_end = ps_spill[:, 0:2]
        ps_pick = ps_spill[:, 64:64 + BLOCKS * (SPILL + 1)].rearrange("p (c s) -> p c s", c=BLOCKS)
        ps_back = ps_score[:, :]
        ps_pf = ps_score[:, 128:128 + BLOCKS * H * SPILL]

        x_in, w_in, iotas, consts, w_ready = (sem(n) for n in ("x_in", "w_in", "iotas", "consts", "w_ready"))
        adj_in = [sem("adj_in0"), sem("adj_in1")]
        early_gathered = [sem("early_gathered0"), sem("early_gathered1")]
        late_gathered = [sem("late_gathered0"), sem("late_gathered1")]
        spill_gathered = [sem("spill_gathered0"), sem("spill_gathered1")]
        stored = [sem("stored0"), sem("stored1")]
        names = ("hit_ready packed cand_done idx_ready idx_kept spill_n_ready end_ready map_ready mapT_ready maps_done "
                 "spill_idx_ready scored spread_ready back_ready neg_max_ready prob_ready pf_ready "
                 "pf_done part_weighed weighted y_ready y_read var_ready rstd_ready x1_ready x1T_ready x1T_copied wh_ready "
                 "wh_copied x1_kept").split()
        S = {n: sem(n) for n in names}
        (hit_ready, packed, cand_done, idx_ready, idx_kept, spill_n_ready, end_ready, map_ready, mapT_ready, maps_done,
         spill_idx_ready, scored, spread_ready, back_ready, neg_max_ready, prob_ready, pf_ready,
         pf_done, part_weighed, weighted, y_ready, y_read, var_ready, rstd_ready, x1_ready, x1T_ready, x1T_copied, wh_ready,
         wh_copied, x1_kept) = (S[n] for n in names)
        T = {n: sem("second_" + n) for n in ("end_copied map_ready mapT_ready mapT_copied spread_ready back_ready e_ready "
                                             "prob_ready pf_ready weighted y_ready y_read low_ready exp_ready "
                                             "var_ready rstd_ready out_ready idx_copied").split()}
        gathered2 = [sem("second_gathered0"), sem("second_gathered1")]
        out_stored = [sem("out_stored0"), sem("out_stored1")]
        D0, D1 = ({n: sem(f"dense{layer}_{n}") for n in (
            "adj_in tile_in key_in values_in xT_ready xT_copied scored score_copied neg_max_ready prob_ready block_ready "
            "turned turned_copied summed added pass_done var_ready rstd_ready x1_ready x1T_ready x1T_copied "
            "wh_ready wh_copied stored low_ready exp_ready out_ready").split()} for layer in range(2))
        bad_ready, bad_summed, flag_ready = (sem(n) for n in ("bad_ready", "bad_summed", "flag_ready"))
        settled = sem("settled")
        dve_chain = sem("dve_chain")
        act_chain = sem("act_chain")

        def tiles_of(engine, step, first=4):
            with engine.Fori(0, (TILES - first) // 2) as q:
                for b in range(2):
                    step(q * 2 + (first + b), q + (first + b) // 2, b)

        def sparse(engine):
            engine.wait_ge(flag_ready, 1)
            return engine.value_load(flag[0:1, 0:1], min_val=0, max_val=1)

        def turns(engine, step):
            engine.sem_inc(settled, 1)
            with engine.Fori(0, GROUPS) as g:
                step(g)

        def dense_loads(sp):
            sp.dma_start(x_sb[:, :, :], ks.rearrange("(t p) d -> p t d", p=P)).then_inc(D0["values_in"], 16)
            with sp.Fori(0, TILES) as t:
                sp.wait_ge(D0["pass_done"], t + 1)
                sp.sem_inc(settled, 1)
                sp.dma_start(adj_row, adj[bass.ds(t * P, P), :]).then_inc(D0["adj_in"], 16)
                sp.dma_start(z[:, 0, :], x[bass.ds(t * P, P), :]).then_inc(D0["tile_in"], 16)
                sp.wait_ge(D0["wh_copied"], t + 2)
                sp.sem_inc(settled, 1)
                sp.dma_start(wh_dram[bass.ds(t * P, P), :], wh_sb[:, 0, 0:ROW]).then_inc(D0["stored"], 16)
                sp.dma_start(dst_dram[:, bass.ds(t * P, P)], dst_sb).then_inc(D0["stored"], 16)
                sp.dma_start(x1_dram[bass.ds(t * P, P), :], x1[:, 0, :]).then_inc(D0["stored"], 16)
                sp.wait_ge(D0["stored"], t * 48 + 48)
                sp.sem_inc(settled, 1)
            sp.wait_ge(D0["pass_done"], TILES + 1)
            sp.dma_start(x_sb[:, :, :], wh_dram[:, 0:D].rearrange("(t p) d -> p t d", p=P)).then_inc(D1["values_in"], 16)
            with sp.Fori(0, TILES) as t:
                for h in range(H):
                    sp.wait_ge(D1["pass_done"], t * H + h + 1)
                    sp.sem_inc(settled, 1)
                    if h == 0:
                        sp.dma_start(z[:, 0, :], x1_dram[bass.ds(t * P, P), :]).then_inc(D1["tile_in"], 16)
                    sp.dma_start(adj_row, adj[bass.ds(t * P, P), :]).then_inc(D1["adj_in"], 16)
                    sp.dma_start(key_row, dst_dram[h:h + 1, :].to_broadcast([P, N])).then_inc(D1["key_in"], 16)
                sp.wait_ge(D1["out_ready"], t + 2)
                sp.sem_inc(settled, 1)
                sp.dma_start(out[bass.ds(t * P, P), :], x1[:, 0, :]).then_inc(D1["stored"], 16)
                sp.wait_ge(D1["stored"], t * 16 + 16)
                sp.sem_inc(settled, 1)
            sp.wait_ge(D1["stored"], 16 * TILES)

        def dense_scalar(act):
            def turn(S, src, dst, m):
                act.wait_ge(S["turned"], m + 1)
                act.activation(blocks.rearrange("p a d -> p (a d)"), src, ACT.Copy).then_inc(S["block_ready"], 1)
                act.wait_ge(S["turned"], m + 2)
                act.activation(dst, ps_toT[:, :], ACT.Copy).then_inc(S["turned_copied"], 1)

            def exp_and_turn(S, n, base):
                act.wait_ge(S["neg_max_ready"], n + 2)
                act.activation(row, row, ACT.Exp, bias=neg_max[:, 0, :],
                               accum_out=rsum[:, 0, 0:1]).then_inc(S["prob_ready"], 1)
                act.wait_ge(S["prob_ready"], n + 2)

                def values_turn(g):
                    act.wait_ge(S["summed"], n * GROUPS + g + 1)
                    turn(S, row[:, bass.ds(g * 512, 512)], turned_sb.rearrange("p a d -> p (a d)"), n * GROUPS + g + base)

                turns(act, values_turn)

            def root(S, n):
                act.wait_ge(S["var_ready"], n + 2)
                act.activation(ln_var[:, :], mv[:, 0, 1:2], ACT.Ln, bias=eps_sb[:, :]).then_inc(act_chain, 1)
                act.wait_ge(act_chain, n + (TILES + 1 + (TILES if S is D1 else 0)))
                act.activation(rstd[:, 0, :], ln_var[:, :], ACT.Exp, scale=-0.5).then_inc(S["rstd_ready"], 1)

            act.wait_ge(D0["values_in"], 16)
            turns(act, lambda g: turn(D0, x_sb[:, bass.ds(g * 4, 4), :].rearrange("p a d -> p (a d)"),
                                      key_row[:, bass.ds(g * 512, 512)], g))
            with act.Fori(0, TILES) as t:
                act.wait_ge(D0["xT_ready"], t + 2)
                act.activation(x1T[:, :], ps_wh[:, 0:P], ACT.Copy).then_inc(D0["xT_copied"], 1)
                exp_and_turn(D0, t, GROUPS)
                root(D0, t)
                act.wait_ge(D0["x1T_ready"], t + 2)
                act.activation(x1T[:, :], ps_wh[:, 0:P], ACT.Copy).then_inc(D0["x1T_copied"], 1)
                act.wait_ge(D0["wh_ready"], t + 2)
                act.activation(src_all[:, bass.ds(t, 1), :].rearrange("p a h -> p (a h)"), ps_wh[:, ROW:EXT], ACT.Copy)
                act.activation(dst_sb, ps_xs[0:H, 0:P], ACT.Copy)
                act.activation(wh_sb[:, 0, 0:ROW], ps_wh[:, 0:ROW], ACT.Copy).then_inc(D0["wh_copied"], 1)
            with act.Fori(0, TILES) as t:
                for h in range(H):
                    exp_and_turn(D1, t * H + h, 0)
                act.wait_ge(D1["low_ready"], t + 2)
                act.activation(elu_exp[:, :], elu_low[:, :], ACT.Exp).then_inc(D1["exp_ready"], 1)
                root(D1, t)

        def dense_vector(dve, restart_chain, link, at):
            def softmax_and_sum(S, n):
                link(nc.vector.scalar_tensor_tensor(row, row, LEAK, row, ALU.mult, ALU.max))
                link(nc.vector.scalar_tensor_tensor(row, adj_row, 0.0, row, ALU.is_gt, ALU.mult))
                link(nc.vector.tensor_scalar(masked_row, adj_row, 0.0, MASKED, ALU.is_le, ALU.mult))
                link(nc.vector.tensor_tensor(row, row, masked_row, ALU.add))
                link(nc.vector.tensor_reduce(rmax[:, 0:1], row, AX, ALU.max))
                nc.vector.tensor_scalar(neg_max[:, 0, :], rmax[:, 0:1], -1.0, None, ALU.mult).then_inc(S["neg_max_ready"], 1)
                link(nc.vector.memset(acc, 0.0))
                dve.wait_ge(S["prob_ready"], n + 2)
                link(nc.vector.reciprocal(rinv[:, 0, 0:1], rsum[:, 0, 0:1]))

                def add(g):
                    dve.wait_ge(S["summed"], n * GROUPS + g + 2)
                    nc.vector.tensor_tensor(acc, acc, ps_y[:, 0:D], ALU.add).then_inc(S["added"], 1)
                    dve.wait_ge(S["added"], n * GROUPS + g + 2)

                turns(dve, add)

            def norm(S, n, done):
                link(nc.vector.bn_stats(stats[:, :], z[:, 1, :]))
                nc.vector.bn_aggr(mv[:, 0, :], stats[:, :]).then_inc(S["var_ready"], 1)
                dve.wait_ge(S["rstd_ready"], n + 2)
                nc.vector.tensor_scalar(x1[:, 0, :], z[:, 1, :], mv[:, 0, 0:1], rstd[:, 0, :], ALU.subtract,
                                        ALU.mult).then_inc(done, 1)

            with dve.Fori(0, TILES) as t:
                restart_chain()

                def copy_scores(c):
                    dve.wait_ge(D0["scored"], t * GROUPS + c + 2)
                    nc.vector.tensor_copy(row[:, bass.ds(c * 512, 512)], ps_back[:, :]).then_inc(D0["score_copied"], 1)

                turns(dve, copy_scores)
                dve.wait_ge(D0["score_copied"], t * GROUPS + GROUPS + 1)
                dve.wait_ge(D0["adj_in"], t * 16 + 16)
                softmax_and_sum(D0, t)
                dve.wait_ge(D0["tile_in"], t * 16 + 16)
                link(nc.vector.scalar_tensor_tensor(z[:, 1, :], acc, rinv[:, 0, 0:1], z[:, 0, :], ALU.mult, ALU.add))
                norm(D0, t, D0["x1_ready"])
                dve.wait_ge(D0["x1T_copied"], t + 2)
                link(nc.vector.memset(score_spill[:, :], 0.0))
                nc.vector.memset(score_spill[:, :], 0.0).then_inc(D0["pass_done"], 1)
            dve.wait_ge(D0["wh_copied"], TILES + 1)
            with dve.Fori(0, TILES) as t:
                for h in range(H):
                    restart_chain()
                    n = t * H + h
                    dve.wait_ge(D1["key_in"], n * 16 + 16)
                    dve.wait_ge(D1["adj_in"], n * 16 + 16)
                    link(nc.vector.tensor_copy(spill_n[:, :], at(src_all, t)[:, h:h + 1]))
                    link(nc.vector.tensor_scalar(row, key_row, spill_n[:, :], None, ALU.add))
                    softmax_and_sum(D1, n)
                    link(nc.vector.tensor_scalar(hn[:, h * HD:(h + 1) * HD], acc[:, h * HD:(h + 1) * HD],
                                                 rinv[:, 0, 0:1], None, ALU.mult))
                    nc.vector.memset(score_spill[:, :], 0.0).then_inc(D1["pass_done"], 1)
                restart_chain()
                nc.vector.tensor_scalar(elu_low[:, :], hn[:, :], 0.0, None, ALU.min).then_inc(D1["low_ready"], 1)
                dve.wait_ge(D1["exp_ready"], t + 2)
                link(nc.vector.scalar_tensor_tensor(hn[:, :], hn[:, :], 0.0, elu_exp[:, :], ALU.max, ALU.add))
                dve.wait_ge(D1["tile_in"], t * 16 + 16)
                link(nc.vector.scalar_tensor_tensor(z[:, 1, :], hn[:, :], -1.0, z[:, 0, :], ALU.add, ALU.add))
                norm(D1, t, D1["out_ready"])
                link(nc.vector.memset(score_spill[:, :], 0.0))

        def dense_tensor(pe):
            mm = nc.tensor.matmul

            def turn(S, m):
                pe.wait_ge(S["block_ready"], m + 2)
                pe.wait_ge(S["turned_copied"], m + 1)
                for k in range(4):
                    last = nc.tensor.transpose(ps_toT[:, k * P:(k + 1) * P], blocks[:, k, :], ident[:, :])
                last.then_inc(S["turned"], 1)

            def sum_values(S, n, base):
                def group(g):
                    turn(S, n * GROUPS + g + base)
                    pe.wait_ge(S["turned_copied"], n * GROUPS + g + (base + 1) + 1)
                    pe.wait_ge(S["added"], n * GROUPS + g + 1)
                    for k in range(4):
                        last = mm(ps_y[:, 0:D], turned_sb[:, k, :],
                                  x_sb[:, bass.ds(g * 4 + k, 1), :].rearrange("p a d -> p (a d)"),
                                  start=(k == 0), stop=(k == 3))
                    last.then_inc(S["summed"], 1)

                turns(pe, group)

            turns(pe, lambda g: turn(D0, g))
            pe.wait_ge(D0["turned_copied"], GROUPS + 1)
            with pe.Fori(0, TILES) as t:
                pe.wait_ge(D0["tile_in"], t * 16 + 16)
                pe.wait_ge(D0["wh_copied"], t + 1)
                nc.tensor.transpose(ps_wh[:, 0:P], z[:, 0, :], ident[:, :]).then_inc(D0["xT_ready"], 1)
                pe.wait_ge(D0["xT_copied"], t + 2)

                def scores(c):
                    pe.wait_ge(D0["score_copied"], t * GROUPS + c + 1)
                    mm(ps_back[:, :], x1T[:, :], key_row[:, bass.ds(c * 512, 512)], start=True,
                       stop=True).then_inc(D0["scored"], 1)

                turns(pe, scores)
                sum_values(D0, t, GROUPS)
                pe.wait_ge(D0["x1_ready"], t + 2)
                nc.tensor.transpose(ps_wh[:, 0:P], x1[:, 0, :], ident[:, :]).then_inc(D0["x1T_ready"], 1)
                pe.wait_ge(D0["x1T_copied"], t + 2)
                mm(ps_xs[0:H, 0:P], w_ext[:, D:ROW], x1T[:, :], start=True, stop=True)
                mm(ps_wh[:, 0:EXT], x1T[:, :], w_ext[:, :], start=True, stop=True).then_inc(D0["wh_ready"], 1)
            pe.wait_ge(D1["values_in"], 16)
            with pe.Fori(0, TILES) as t:
                for h in range(H):
                    sum_values(D1, t * H + h, 0)

        block = ctx.enter_context(nc.Block())

        @block.sync
        def _(sp):
            sp.dma_start(w_ext[:, 0:D], W).then_inc(w_in, 16)
            sp.dma_start(a_sb, a.to_broadcast([P, H, 2 * HD])).then_inc(w_in, 16)

            def load_adj(t, half, b):
                sp.dma_start(adj_sb[:, b, 0:N // 2], adj[bass.ds(t * P, P), 0:N // 2]).then_inc(adj_in[b], 16)
                sp.wait_ge(adj_in[b], half * 32 + 16)
                if not isinstance(t, int) or t >= 4:
                    sp.sem_inc(settled, 1)
                    sp.wait_ge(spill_gathered[b], half * (16 * BLOCKS) - 16 * BLOCKS)
                sp.sem_inc(settled, 1)
                sp.dma_start(adj_sb[:, b, N // 2:N], adj[bass.ds(t * P, P), N // 2:N]).then_inc(adj_in[b], 16)

            def store_wh(t, b):
                sp.wait_ge(wh_copied, t + 1)
                sp.dma_start(wh_dram[bass.ds(t * P, P), :], wh_sb[:, b, 0:ROW]).then_inc(stored[b], 16)

            load_adj(0, 0, 0)
            sp.dma_start(x_sb[:, :, :], x_v).then_inc(x_in, 16)
            load_adj(1, 0, 1)

            def step(t, half, b):
                sp.wait_ge(hit_ready, t - 1)
                load_adj(t, half, b)

            step(2, 1, 0)
            step(3, 1, 1)

            def both(t, half, b):
                step(t, half, b)
                store_wh(t - 6, b)

            step(4, 2, 0)
            step(5, 2, 1)
            tiles_of(sp, both, 6)
            for t in range(TILES - 6, TILES):
                store_wh(t, t % 2)

            with sp.If(sparse(sp) == 0):
                def store_out(t, half, b):
                    sp.wait_ge(T["out_ready"], t + 1)
                    sp.dma_start(out[bass.ds(t * P, P), :], x1[:, b, :]).then_inc(out_stored[b], 16)

                tiles_of(sp, store_out, 0)
                for b in range(2):
                    sp.wait_ge(out_stored[b], 16 * (TILES // 2))
            with sp.Else():
                dense_loads(sp)

        @block.gpsimd
        def _(pool):
            nc.gpsimd.iota(pos_high[:, :], [[1, POS // 256]], base=0, channel_multiplier=0,
                           allow_small_or_imprecise_dtypes=True).then_inc(iotas, 1)
            nc.gpsimd.iota(pos_low[:, :], [[1, 256]], base=0, channel_multiplier=0,
                           allow_small_or_imprecise_dtypes=True).then_inc(iotas, 1)
            nc.gpsimd.iota(fold_base[:, :, :], [[POS, FOLD], [0, MULTI]], base=N, channel_multiplier=0,
                           allow_small_or_imprecise_dtypes=True).then_inc(iotas, 1)
            nc.gpsimd.iota(pos_iota[:, :], [[1, BLOCKS * P]], base=0, channel_multiplier=0,
                           allow_small_or_imprecise_dtypes=True).then_inc(iotas, 1)
            nc.gpsimd.iota(row_iota[:, :], [[P, BLOCKS]], base=0, channel_multiplier=1,
                           allow_small_or_imprecise_dtypes=True).then_inc(iotas, 1)

            def gather(t, half, b):
                pool.wait_ge(idx_ready, t + 1)
                if not isinstance(t, int) or t >= 2:
                    pool.wait_ge(scored, t - 1)
                    pool.wait_ge(part_weighed, t - 1)
                pool.sem_inc(settled, 1)
                for s in range(PRIMARY):
                    if s == PART and (not isinstance(t, int) or t >= 2):
                        pool.wait_ge(weighted, t - 1)
                        pool.sem_inc(settled, 1)
                    pool.indirect_dma_start(
                        out=keys[:, b, s, 0:D], out_offset=None, in_=ks,
                        in_offset=bass.IndirectOffsetOnAxis(ap=idx[:, b, s:s + 1], axis=0)
                    ).then_inc(early_gathered[b] if s < EARLY else late_gathered[b], 16)
                pool.wait_ge(spill_idx_ready, t + 1)
                pool.sem_inc(settled, 1)
                for s in range(PRIMARY, GATHERS):
                    pool.indirect_dma_start(
                        out=keys[:, b, s, 0:D], out_offset=None, in_=ks,
                        in_offset=bass.IndirectOffsetOnAxis(ap=idx[:, b, s:s + 1], axis=0)
                    ).then_inc(spill_gathered[b], 16)

            gather(0, 0, 0)
            gather(1, 0, 1)
            tiles_of(pool, gather, 2)

            with pool.If(sparse(pool) == 0):
                for b in range(2):
                    pool.wait_ge(stored[b], 16 * (TILES // 2))
                pool.wait_ge(y_ready, TILES)

                def gather2(t, half, b):
                    pool.wait_ge(T["idx_copied"], t + 1)
                    if not isinstance(t, int) or t >= 2:
                        pool.wait_ge(T["y_ready"], t - 1)
                    pool.sem_inc(settled, 1)
                    for s in range(GATHERS):
                        pool.indirect_dma_start(
                            out=keys[:, b, s, :], out_offset=None, in_=wh_dram,
                            in_offset=bass.IndirectOffsetOnAxis(ap=idx[:, b, s:s + 1], axis=0)).then_inc(gathered2[b], 16)

                gather2(0, 0, 0)
                gather2(1, 0, 1)
                tiles_of(pool, gather2, 2)
            with pool.Else():
                pool.wait_ge(flag_ready, 1)

        @block.scalar
        def _(act):
            act.preload_act_table_set("natural_log_exp_and_others")

            def hits(t, half, b):
                act.wait_ge(adj_in[b], half * 32 + 32)
                if not isinstance(t, int) or t >= 2:
                    act.wait_ge(packed, t - 1)
                act.activation(hit[:, b, :], adj_sb[:, b, :], ACT.Relu,
                               accum_out=edge_sum[:, bass.ds(t, 1)]).then_inc(hit_ready, 1)

            def root(t, half, b):
                act.wait_ge(var_ready, t + 1)
                act.activation(ln_var[:, :], mv[:, b, 1:2], ACT.Ln, bias=eps_sb[:, :]).then_inc(act_chain, 1)
                act.wait_ge(act_chain, t + 1)
                act.activation(rstd[:, b, :], ln_var[:, :], ACT.Exp, scale=-0.5).then_inc(rstd_ready, 1)

            def keep_x1(t, half, b):
                act.wait_ge(x1_ready, t + 1)
                act.activation(x_sb[:, bass.ds(t, 1), :].rearrange("p a d -> p (a d)"), x1[:, b, :],
                               ACT.Copy).then_inc(x1_kept, 1)
                act.wait_ge(x1T_ready, t + 1)
                act.activation(x1T[:, :], ps_wh[:, 0:P], ACT.Copy).then_inc(x1T_copied, 1)

            def keep_wh(t, half, b):
                act.wait_ge(wh_ready, t + 1)
                if not isinstance(t, int) or t >= 2:
                    act.wait_ge(stored[b], half * 16)
                act.activation(src_all[:, bass.ds(t, 1), :].rearrange("p a h -> p (a h)"), ps_wh[:, ROW:EXT], ACT.Copy)
                act.activation(wh_sb[:, b, 0:ROW], ps_wh[:, 0:ROW], ACT.Copy).then_inc(wh_copied, 1)

            def keep_idx(t, half, b):
                act.wait_ge(spill_idx_ready, t + 1)
                act.activation(idx_all[:, bass.ds(t, 1), :].rearrange("p a n -> p (a n)"), idx[:, b, :],
                               ACT.Copy).then_inc(idx_kept, 1)

            def softmax(t, half, b):
                act.wait_ge(neg_max_ready, t + 1)
                act.activation(prob[:, b, 0, :], score[:, :], ACT.Exp, bias=neg_max[:, b, :],
                               accum_out=rsum[:, b, 0:1]).then_inc(prob_ready, 1)

            def copy_map(t, half, b):
                act.wait_ge(mapT_ready, t + 1)
                if not isinstance(t, int) or t >= 2:
                    act.wait_ge(y_ready, t - 1)
                act.activation(to_row[:, b, :], ps_toT[:, 0:BLOCKS * P], ACT.Copy).then_inc(maps_done, 1)

            def weigh(t, half, b, between=None):
                if not isinstance(t, int) or t >= 1:
                    act.wait_ge(y_ready, t)
                act.wait_ge(prob_ready, t + 1)
                for s in range(PRIMARY):
                    if s == PART and between is not None:
                        keep_wh(*between)
                    done = act.activation(weighed[:, s, :], keys[:, b, s, 0:D], ACT.Copy, scale=prob[:, b, 0, s:s + 1])
                    if s == PART - 1:
                        done.then_inc(part_weighed, 1)
                act.wait_ge(pf_done, t + 1)
                for c in range(BLOCKS):
                    last = act.activation(weighed[:, PRIMARY + c, :], keys[:, b, PRIMARY + c, 0:D], ACT.Copy,
                                          scale=prob_spill[:, b, c, 0:1])
                last.then_inc(weighted, 1)

            def step(t, half, b, lists=True, attend=True, end=True):
                if end:
                    weigh(t - 2, half - 1, b, None if isinstance(t, int) and t == 2 else (t - 3, half - 2 + b, 1 - b))
                if not isinstance(t, int) or t < TILES - 2:
                    hits(t + 2, half + 1, b)
                if lists:
                    copy_map(t, half, b)
                if end:
                    root(t - 2, half - 1, b)
                if lists:
                    keep_idx(t, half, b)
                if attend:
                    softmax(t - 1, half - 1 + b, 1 - b)
                if end:
                    keep_x1(t - 2, half - 1, b)

            act.wait_ge(consts, 1)
            hits(0, 0, 0)
            hits(1, 0, 1)
            step(0, 0, 0, attend=False, end=False)
            step(1, 0, 1, end=False)
            step(2, 1, 0)
            step(3, 1, 1)
            with act.Fori(0, (TILES - 6) // 2) as q:
                for b in range(2):
                    step(q * 2 + (4 + b), q + 2, b)
            step(TILES - 2, TILES // 2 - 1, 0)
            step(TILES - 1, TILES // 2 - 1, 1)
            step(TILES, TILES // 2, 0, lists=False)
            step(TILES + 1, TILES // 2, 1, lists=False, attend=False)
            keep_wh(TILES - 1, TILES // 2 - 1, 1)

            with act.If(sparse(act) == 0):
                def copy_idx(t, half, b):
                    if not isinstance(t, int) or t >= 2:
                        act.wait_ge(gathered2[b], half * (16 * GATHERS))
                    act.activation(idx[:, b, :], idx_all[:, bass.ds(t, 1), :].rearrange("p a n -> p (a n)"),
                                   ACT.Copy).then_inc(T["idx_copied"], 1)

                def copy_ends(t, half, b):
                    act.activation(spill_end[:, b, :], end_all[:, bass.ds(t, 1), :].rearrange("p a n -> p (a n)"), ACT.Copy).then_inc(T["end_copied"], 1)

                def copy_map2(t, half, b):
                    act.wait_ge(T["mapT_ready"], t + 1)
                    act.activation(to_row[:, b, :], ps_toT[:, 0:BLOCKS * P], ACT.Copy).then_inc(T["mapT_copied"], 1)

                def softmax2(t, half, b):
                    act.wait_ge(T["e_ready"], t + 1)
                    act.activation(prob[:, b, :, :], e[:, :, :], ACT.Exp).then_inc(T["prob_ready"], 1)

                def finish2(t, half, b):
                    act.wait_ge(T["low_ready"], t + 1)
                    act.activation(elu_exp[:, :], elu_low[:, :], ACT.Exp).then_inc(T["exp_ready"], 1)
                    act.wait_ge(T["var_ready"], t + 1)
                    act.activation(ln_var[:, :], mv[:, b, 1:2], ACT.Ln, bias=eps_sb[:, :]).then_inc(act_chain, 1)
                    act.wait_ge(act_chain, t + (TILES + 1))
                    act.activation(rstd[:, b, :], ln_var[:, :], ACT.Exp, scale=-0.5).then_inc(T["rstd_ready"], 1)

                def step2(t, half, b, maps=True, attend=True, end=True):
                    if maps:
                        copy_idx(t, half, b)
                        if not isinstance(t, int) or t >= 2:
                            act.wait_ge(T["map_ready"], t - 1)
                        copy_ends(t, half, b)
                        copy_map2(t, half, b)
                    if attend:
                        softmax2(t - 1, half - 1 + b, 1 - b)
                    if end:
                        finish2(t - 2, half - 1, b)

                act.wait_ge(idx_kept, TILES)
                for b in range(2):
                    act.wait_ge(late_gathered[b], 16 * (PRIMARY - EARLY) * (TILES // 2))
                    act.wait_ge(early_gathered[b], 16 * EARLY * (TILES // 2))
                    act.wait_ge(spill_gathered[b], 16 * BLOCKS * (TILES // 2))
                step2(0, 0, 0, attend=False, end=False)
                step2(1, 0, 1, end=False)
                step2(2, 1, 0)
                step2(3, 1, 1)
                tiles_of(act, step2)
                step2(TILES, TILES // 2, 0, maps=False)
                finish2(TILES - 1, TILES // 2 - 1, 1)
            with act.Else():
                dense_scalar(act)

        @block.vector
        def _(dve):
            count = [0]
            dot_written = [0] * PRIMARY

            def restart_chain():
                dve.sem_clear(dve_chain)
                count[0] = 0

            def mark(ins):
                count[0] += 1
                ins.then_inc(dve_chain, 1)

            def link(ins):
                mark(ins)
                dve.wait_ge(dve_chain, count[0])

            def at(buf, t):
                return buf[:, bass.ds(t, 1), :].rearrange("p a n -> p (a n)")

            def spread_over(ap, n, d):
                return ap.rearrange("p (a d) -> p a d", a=1).to_broadcast([P, n, d])

            def each(ap, n, d):
                return ap.rearrange("p (n a) -> p n a", a=1).to_broadcast([P, n, d])

            nc.vector.memset(ones[:, :], 1.0)
            nc.vector.memset(eps_sb[:, :], EPS)
            dve.wait_ge(iotas, 5)
            link(nc.vector.tensor_scalar(ident[:, :], pos_iota[:, 0:P], row_iota[:, 0:1], None, ALU.is_equal))
            link(nc.vector.tensor_scalar(upper[:, 0, :], pos_iota[:, 0:P], row_iota[:, 0:1], None, ALU.is_gt))
            link(nc.vector.tensor_scalar(upper[:, 1, :], pos_iota[:, 0:P], row_iota[:, 0:1], None, ALU.is_ge))
            for k in range(FOLD):
                nc.vector.tensor_scalar(scaled_id[:, k, :], ident[:, :], float(POS * 2 ** k), None, ALU.mult)
                nc.vector.memset(fold_bit[:, k, :], POS * 2 ** k)
            nc.vector.tensor_scalar(scaled_id[:, FOLD, :], ident[:, :], 256.0, None, ALU.mult)
            nc.vector.tensor_scalar(scaled_id[:, FOLD + 1, :], ident[:, :], 1.0, None, ALU.mult).then_inc(consts, 1)
            dve.wait_ge(w_in, 32)
            for k, lo in ((0, HD), (1, 0)):
                link(nc.vector.tensor_tensor(wa, w_ext[:, 0:D].rearrange("p (h k) -> p h k", h=H),
                                             a_sb[:, :, lo:lo + HD], ALU.mult))
                link(nc.vector.tensor_reduce(w_ext[:, D + k * H:D + (k + 1) * H], wa, AX, ALU.add))
            nc.vector.memset(score_spill[:, :], 0.0).then_inc(w_ready, 1)

            def candidates(t, half, b):
                dve.wait_ge(packed, t + 1)
                dve.sem_inc(settled, 1)
                for c in range(NCH):
                    at_c = c * CHUNK % 512
                    last = nc.vector.max(cand[:, 8 * c:8 * c + 8], ps_code[c * CHUNK // 512][:, at_c:at_c + CHUNK])
                last.then_inc(cand_done, 1)

            def largest(dst, src, between=None):
                for r in range(0, SLOTS, 8):
                    for k, step in enumerate((lambda: nc.vector.max(dst[:, r:r + 8], src),
                                              lambda: nc.vector.match_replace(src, dst[:, r:r + 8], src, 0.0))):
                        if r + 8 * k < SLOTS:
                            count[0] += 1
                            written = count[0]
                            step().then_inc(dve_chain, 1)
                            if between is not None:
                                between(r // 4 + k)
                            dve.wait_ge(dve_chain, written)

            def sort_codes(t, half, b, prev=None):
                candidates(t, half, b)
                dve.wait_ge(cand_done, t + 1)
                dve.sem_inc(settled, 1)
                if prev is None:
                    largest(codes[:, :], cand[:, :])
                else:
                    late_gathers(*prev)
                    largest(codes[:, :], cand[:, :],
                            lambda i: dot(EARLY + i - 1, prev[0], prev[2]) if 1 <= i < PRIMARY - EARLY - 2 else None)

            def lists(t, half, b, prev=None, last=None):
                code_bits = codes[:, :].bitcast(I32)
                exponent_of_pos = 127 + POS.bit_length() - 1
                mark(nc.vector.tensor_scalar(top_bit[:, :], code_bits, EXPONENT, None, ALU.bitwise_and))
                mark(nc.vector.tensor_scalar(top_k[:, :], code_bits, 23, None, ALU.logical_shift_right))
                link(nc.vector.tensor_copy(code_int[:, :], codes[:, :]))
                mark(nc.vector.tensor_tensor(rest[:, :], codes[:, :], top_bit[:, :].bitcast(F32), ALU.subtract))
                mark(nc.vector.tensor_scalar(top_base[:, :], top_k[:, :], float(POS), float(N - exponent_of_pos * POS),
                                             ALU.mult, ALU.add))
                link(nc.vector.tensor_scalar(code_pos[:, :], code_int[:, :], POS - 1, None, ALU.bitwise_and))
                mark(nc.vector.max(multi[:, :], rest[:, :]))
                link(nc.vector.tensor_tensor(top_col[:, :], top_base[:, :], code_pos[:, :], ALU.add))
                mark(nc.vector.scalar_tensor_tensor(found[:, 0:SLOTS], codes[:, :], float(POS), top_col[:, :],
                                                    ALU.is_ge, ALU.mult))
                link(nc.vector.tensor_copy(multi_int[:, :], multi[:, :]))
                by_fold = spread_over(multi_int[:, :], FOLD, MULTI)
                mark(nc.vector.scalar_tensor_tensor(grid_cols[:, :, :], by_fold, POS - 1, fold_base[:, :, :],
                                                    ALU.bitwise_and, ALU.bitwise_or))
                link(nc.vector.tensor_tensor(grid_bits[:, :, :], fold_bit[:, :, :], by_fold, ALU.bitwise_and))
                link(nc.vector.scalar_tensor_tensor(
                    found[:, SLOTS:SLOTS + FOLD * MULTI], grid_bits[:, :, :].rearrange("p k s -> p (k s)"), 0.0,
                    grid_cols[:, :, :].rearrange("p k s -> p (k s)"), ALU.is_gt, ALU.mult))
                if last is not None:
                    spill_prob(*last)
                if prev is None:
                    largest(cols[:, b, 0:SLOTS], found[:, :])
                else:
                    early_gathers(*prev)
                    largest(cols[:, b, 0:SLOTS], found[:, :],
                            lambda s: dot(s, prev[0], prev[2]) if s < EARLY else None)
                nc.vector.scalar_tensor_tensor(spill_gt[:, :], cols[:, b, PRIMARY:SLOTS], 0.0, ones[:, :], ALU.is_gt,
                                               ALU.mult, accum_out=spill_n[:, :]).then_inc(spill_n_ready, 1)
                if not isinstance(t, int) or t >= 2:
                    dve.wait_ge(idx_kept, t - 1)
                    dve.wait_ge(early_gathered[b], half * (16 * EARLY))
                    dve.wait_ge(late_gathered[b], half * (16 * (PRIMARY - EARLY)))
                    dve.wait_ge(spill_gathered[b], half * (16 * BLOCKS))
                nc.vector.tensor_scalar(idx[:, b, 0:PRIMARY], cols[:, b, 0:PRIMARY], float(-N), 0.0, ALU.add,
                                        ALU.max).then_inc(idx_ready, 1)
                link(nc.vector.tensor_scalar(at(neg_all, t), cols[:, b, 0:SLOTS], 0.0, MASKED, ALU.is_le, ALU.mult))

            def spill_map(t, half, b):
                dve.wait_ge(end_ready, t + 1)
                mark(nc.vector.tensor_copy(spill_end[:, b, :], ps_end[:, 0:2]))
                link(nc.vector.tensor_copy(at(end_all, t), ps_end[:, 0:2]))
                make_map(b).then_inc(map_ready, 1)

            def make_map(b):
                link(nc.vector.tensor_scalar(below_end[:, :], pos_iota[:, :], spill_end[:, b, 1:2], None, ALU.is_lt))
                return nc.vector.scalar_tensor_tensor(to_spill[:, b, :], pos_iota[:, :], spill_end[:, b, 0:1],
                                                      below_end[:, :], ALU.is_ge, ALU.mult)

            def spill_idx(t, half, b, between):
                dve.wait_ge(mapT_ready, t + 1)
                slots = at(slot_all, t)
                mark(nc.vector.scalar_tensor_tensor(slots.rearrange("p (c a) -> p c a", a=1), ps_pick[:, :, SPILL:SPILL + 1],
                                                    -1.0, row_iota[:, :].rearrange("p (c a) -> p c a", a=1),
                                                    ALU.mult, ALU.add))
                written = count[0]
                between(PRIMARY - 2)
                dve.wait_ge(dve_chain, written)
                dve.sem_inc(settled, 1)
                mark(make_slot_hot(t, b))
                written = count[0]
                between(PRIMARY - 1)
                dve.wait_ge(dve_chain, written)
                for c in range(BLOCKS):
                    last = nc.vector.scalar_tensor_tensor(picked[:, c, 0:SPILL], slot_hot[:, b, c, :], 1.0,
                                                          ps_pick[:, c, 0:SPILL], ALU.mult, ALU.mult,
                                                          accum_out=col_spill[:, c:c + 1])
                    if c < BLOCKS - 1:
                        mark(last)
                link(last)
                nc.vector.tensor_scalar(idx[:, b, PRIMARY:GATHERS], col_spill[:, :], float(-N), 0.0, ALU.add,
                                        ALU.max).then_inc(spill_idx_ready, 1)

            def make_slot_hot(t, b):
                return nc.vector.tensor_tensor(slot_hot[:, b, :, :], spread_over(pos_iota[:, 0:SPILL], BLOCKS, SPILL),
                                               each(at(slot_all, t), BLOCKS, SPILL), ALU.is_equal)

            def early_gathers(t, half, b):
                dve.wait_ge(early_gathered[b], half * (16 * EARLY) + 16 * EARLY)
                dve.sem_inc(settled, 1)

            def late_gathers(t, half, b):
                dve.wait_ge(late_gathered[b], half * (16 * (PRIMARY - EARLY)) + 16 * (PRIMARY - EARLY))
                dve.sem_inc(settled, 1)

            def dot(s, t, b):
                if s >= 4:
                    dve.wait_ge(dve_chain, dot_written[s - 4])
                nc.vector.scalar_tensor_tensor(prod[:, s % 4, :], keys[:, b, s, 0:D], 1.0, at(x_sb, t), ALU.mult,
                                               ALU.mult, accum_out=score[:, s:s + 1]).then_inc(dve_chain, 1)
                count[0] += 1
                dot_written[s] = count[0]

            def spill_dots(t, half, b):
                dve.wait_ge(dve_chain, count[0])
                dve.wait_ge(spill_gathered[b], half * (16 * BLOCKS) + 16 * BLOCKS)
                dve.sem_inc(settled, 1)
                for c in range(BLOCKS):
                    at_c = (b * BLOCKS + c) * D
                    mark(nc.vector.scalar_tensor_tensor(prod[:, c, :], keys[:, b, PRIMARY + c, 0:D], 1.0,
                                                        ps_xs[:, at_c:at_c + D],
                                                        ALU.mult, ALU.mult, accum_out=score_spill[:, c:c + 1]))
                dve.wait_ge(dve_chain, count[0])
                nc.vector.tensor_tensor(spread[:, :, 0:SPILL], slot_hot[:, b, :, :], each(score_spill[:, :], BLOCKS, SPILL),
                                        ALU.mult).then_inc(scored, 1)

            def mask_primary(t):
                mark(nc.vector.tensor_tensor(score[:, 0:PRIMARY], score[:, 0:PRIMARY], at(neg_all, t)[:, 0:PRIMARY], ALU.add))

            def maxima(t, half, b):
                dve.wait_ge(back_ready, t + 1)
                link(nc.vector.tensor_tensor(score[:, PRIMARY:SLOTS], ps_back[:, 0:SPILL], at(neg_all, t)[:, PRIMARY:SLOTS],
                                             ALU.add))
                link(nc.vector.scalar_tensor_tensor(score[:, :], score[:, :], LEAK, score[:, :], ALU.mult, ALU.max))
                link(nc.vector.tensor_reduce(rmax[:, 0:1], score[:, :], AX, ALU.max))
                restart_chain()
                nc.vector.tensor_scalar(neg_max[:, b, :], rmax[:, 0:1], -1.0, None, ALU.mult).then_inc(neg_max_ready, 1)

            def spill_prob(t, half, b):
                dve.wait_ge(pf_ready, t + 1)
                mark(nc.vector.reciprocal(rinv[:, b, 0:1], rsum[:, b, 0:1]))
                for c in range(BLOCKS):
                    last = nc.vector.scalar_tensor_tensor(
                        picked[:, c, 0:SPILL], slot_hot[:, b, c, :], 1.0, ps_pf[:, c * SPILL:(c + 1) * SPILL],
                        ALU.mult, ALU.mult, accum_out=prob_spill[:, b, c, 0:1])
                    if c < BLOCKS - 1:
                        mark(last)
                last.then_inc(pf_done, 1)

            def norm_stats(zb, b):
                link(nc.vector.bn_stats(stats[:, :], zb))
                return nc.vector.bn_aggr(mv[:, b, :], stats[:, :])

            def norm_a(t, half, b):
                dve.wait_ge(y_ready, t + 1)
                link(nc.vector.scalar_tensor_tensor(z[:, b, :], ps_y[:, 0:D], rinv[:, b, 0:1], at(x_sb, t),
                                                    ALU.mult, ALU.add))
                norm_stats(z[:, b, :], b).then_inc(var_ready, 1)

            def norm_b(t, half, b):
                dve.wait_ge(rstd_ready, t + 1)
                if not isinstance(t, int) or t >= 2:
                    dve.wait_ge(x1_kept, t - 1)
                nc.vector.tensor_scalar(x1[:, b, :], z[:, b, :], mv[:, b, 0:1], rstd[:, b, :], ALU.subtract,
                                        ALU.mult).then_inc(x1_ready, 1)

            def step(t, half, b, lst=True, attend=True, end=True):
                if not attend:
                    restart_chain()
                prev, last = (t - 1, half - 1 + b, 1 - b), (t - 2, half - 1, b)
                if lst:
                    lists(t, half, b, prev if attend else None, last if end else None)
                elif attend:
                    spill_prob(*last)
                    early_gathers(*prev)
                    for s in range(EARLY):
                        dot(s, t - 1, 1 - b)
                elif end:
                    spill_prob(*last)
                more = not isinstance(t, int) or t < TILES - 1
                if more:
                    sort_codes(t + 1, half + b, 1 - b, prev if attend else None)
                elif attend:
                    late_gathers(*prev)
                    for s in range(EARLY, PRIMARY - 3):
                        dot(s, t - 1, 1 - b)
                if lst:
                    spill_map(t, half, b)
                if attend:
                    dot(PRIMARY - 3, t - 1, 1 - b)
                    if not lst:
                        dot(PRIMARY - 2, t - 1, 1 - b)
                        dot(PRIMARY - 1, t - 1, 1 - b)
                if end:
                    norm_a(*last)
                if lst:
                    spill_idx(t, half, b, (lambda s: dot(s, t - 1, 1 - b)) if attend else (lambda s: None))
                if attend:
                    spill_dots(*prev)
                    mask_primary(t - 1)
                if end:
                    norm_b(*last)
                if attend:
                    maxima(*prev)
                if not attend:
                    link(nc.vector.memset(score_spill[:, :], 0.0))

            restart_chain()
            sort_codes(0, 0, 0)
            link(nc.vector.memset(score_spill[:, :], 0.0))
            step(0, 0, 0, attend=False, end=False)
            restart_chain()
            dve.wait_ge(x_in, 16)
            step(1, 0, 1, end=False)
            step(2, 1, 0)
            step(3, 1, 1)
            with dve.Fori(0, (TILES - 6) // 2) as q:
                for b in range(2):
                    step(q * 2 + (4 + b), q + 2, b)
            step(TILES - 2, TILES // 2 - 1, 0)
            step(TILES - 1, TILES // 2 - 1, 1)
            step(TILES, TILES // 2, 0, lst=False)
            step(TILES + 1, TILES // 2, 1, lst=False, attend=False)

            restart_chain()
            link(nc.vector.tensor_scalar(bad[:, 0, :], neg_all[:, :, 0], -1.0, None, ALU.is_lt))
            link(nc.vector.tensor_scalar(bad[:, 1, :], end_all[:, :, 1], float(BLOCKS * P), None, ALU.is_gt))
            link(nc.vector.tensor_scalar(masked_row[:, 0:TILES * SLOTS], neg_all[:, :, :].rearrange("p t s -> p (t s)"),
                                         -1.0, None, ALU.is_gt))
            link(nc.vector.tensor_reduce(bad[:, 3, :], masked_row[:, 0:TILES * SLOTS].rearrange(
                "p (t s) -> p t s", s=SLOTS), AX, ALU.add))
            link(nc.vector.tensor_tensor(bad[:, 2, :], bad[:, 3, :], edge_sum[:, :], ALU.not_equal))
            link(nc.vector.tensor_reduce(bad_n[:, :], bad[:, 0:3, :].rearrange("p k t -> p (k t)"), AX, ALU.add))
            nc.vector.memset(score_spill[:, :], 0.0).then_inc(bad_ready, 1)
            for S in (D0, D1):
                for name in S:
                    if not name.endswith("_in") and name != "stored":
                        dve.sem_inc(S[name], 1)
            dve.wait_ge(bad_summed, 1)
            nc.vector.tensor_scalar(flag[:, :], ps_end[0:1, 0:1], 1.0, None, ALU.min).then_inc(flag_ready, 1)

            with dve.If(sparse(dve) == 0):
                def maps2(t, half, b):
                    dve.wait_ge(T["end_copied"], t + 1)
                    mark(make_slot_hot(t, b))
                    make_map(b).then_inc(T["map_ready"], 1)

                def scores2a(t, half, b):
                    dve.wait_ge(gathered2[b], half * (16 * GATHERS) + 16 * GATHERS)
                    for c in range(BLOCKS):
                        last = nc.vector.tensor_tensor(
                            spread[:, c, :].rearrange("p (h s) -> p h s", h=H), spread_over(slot_hot[:, b, c, :], H, SPILL),
                            each(keys[:, b, PRIMARY + c, D:ROW], H, SPILL), ALU.mult)
                        if c < BLOCKS - 1:
                            mark(last)
                    last.then_inc(T["spread_ready"], 1)
                    link(nc.vector.tensor_tensor(e[:, :, 0:PRIMARY],
                                                 keys[:, b, 0:PRIMARY, D:ROW].rearrange("p s h -> p h s"),
                                                 each(at(src_all, t), H, PRIMARY), ALU.add))

                def scores2b(t, half, b):
                    dve.wait_ge(T["back_ready"], t + 1)
                    link(nc.vector.tensor_tensor(e[:, :, PRIMARY:SLOTS],
                                                 ps_back[:, 0:H * SPILL].rearrange("p (h s) -> p h s", h=H),
                                                 each(at(src_all, t), H, SPILL), ALU.add))
                    link(nc.vector.tensor_tensor(e[:, :, :], e[:, :, :], spread_over(at(neg_all, t), H, SLOTS), ALU.add))
                    flat = e[:, :, :].rearrange("p h s -> p (h s)")
                    link(nc.vector.scalar_tensor_tensor(flat, flat, LEAK, flat, ALU.mult, ALU.max))
                    link(nc.vector.tensor_reduce(rmax[:, :], e[:, :, :], AX, ALU.max))
                    nc.vector.tensor_tensor(e[:, :, :], e[:, :, :], each(rmax[:, :], H, SLOTS),
                                            ALU.subtract).then_inc(T["e_ready"], 1)

                def weigh2(t, half, b):
                    dve.wait_ge(T["prob_ready"], t + 1)
                    by_head = keys[:, b, 0:PRIMARY, 0:D].rearrange("p s (h k) -> p s h k", h=H)
                    nc.vector.tensor_tensor(
                        by_head, by_head,
                        prob[:, b, :, 0:PRIMARY].rearrange("p h (s a) -> p s h a", a=1).to_broadcast([P, PRIMARY, H, HD]),
                        ALU.mult)
                    link(nc.vector.tensor_reduce(rsum[:, b, :], prob[:, b, :, :], AX, ALU.add))
                    link(nc.vector.reciprocal(rinv[:, b, :], rsum[:, b, :]))
                    dve.wait_ge(T["pf_ready"], t + 1)
                    for c in range(BLOCKS):
                        mark(nc.vector.tensor_tensor(
                            picked[:, c, :].rearrange("p (h s) -> p h s", h=H),
                            ps_pf[:, c * H * SPILL:(c + 1) * H * SPILL].rearrange("p (h s) -> p h s", h=H),
                            spread_over(slot_hot[:, b, c, :], H, SPILL), ALU.mult))
                    dve.wait_ge(dve_chain, count[0])
                    by_row = prob_spill[:, b, :, :].rearrange("p c h -> p (c h)")
                    link(nc.vector.tensor_reduce(by_row, picked[:, :, :].rearrange("p c (h s) -> p (c h) s", h=H),
                                                 AX, ALU.add))
                    spill = keys[:, b, PRIMARY:GATHERS, 0:D].rearrange("p c (h k) -> p c h k", h=H)
                    nc.vector.tensor_tensor(
                        spill, spill,
                        prob_spill[:, b, :, :].rearrange("p c (h a) -> p c h a", a=1).to_broadcast([P, BLOCKS, H, HD]),
                        ALU.mult).then_inc(T["weighted"], 1)

                def norm2_a(t, half, b):
                    dve.wait_ge(T["y_ready"], t + 1)
                    link(nc.vector.tensor_tensor(hn[:, :].rearrange("p (h k) -> p h k", h=H),
                                                 ps_y[:, 0:D].rearrange("p (h k) -> p h k", h=H),
                                                 each(rinv[:, b, :], H, HD), ALU.mult))
                    nc.vector.tensor_scalar(elu_low[:, :], hn[:, :], 0.0, None, ALU.min).then_inc(T["low_ready"], 1)

                def norm2_b(t, half, b):
                    dve.wait_ge(T["exp_ready"], t + 1)
                    link(nc.vector.scalar_tensor_tensor(hn[:, :], hn[:, :], 0.0, elu_exp[:, :], ALU.max, ALU.add))
                    link(nc.vector.scalar_tensor_tensor(z[:, b, :], hn[:, :], -1.0, at(x_sb, t), ALU.add, ALU.add))
                    norm_stats(z[:, b, :], b).then_inc(T["var_ready"], 1)
                    dve.wait_ge(T["rstd_ready"], t + 1)
                    if not isinstance(t, int) or t >= 2:
                        dve.wait_ge(out_stored[b], half * 16)
                    nc.vector.tensor_scalar(x1[:, b, :], z[:, b, :], mv[:, b, 0:1], rstd[:, b, :], ALU.subtract,
                                            ALU.mult).then_inc(T["out_ready"], 1)

                def step2(t, half, b, maps=True, attend=True, end=True):
                    restart_chain()
                    prev = (t - 1, half - 1 + b, 1 - b)
                    if maps:
                        maps2(t, half, b)
                    if attend:
                        scores2a(*prev)
                    if end:
                        norm2_a(t - 2, half - 1, b)
                    if attend:
                        scores2b(*prev)
                    if end:
                        norm2_b(t - 2, half - 1, b)
                    if attend:
                        weigh2(*prev)
                    link(nc.vector.memset(score_spill[:, :], 0.0))

                dve.wait_ge(x1_kept, TILES)
                dve.wait_ge(wh_copied, TILES)
                step2(0, 0, 0, attend=False, end=False)
                step2(1, 0, 1, end=False)
                step2(2, 1, 0)
                step2(3, 1, 1)
                tiles_of(dve, step2)
                step2(TILES, TILES // 2, 0, maps=False)
                restart_chain()
                norm2_a(TILES - 1, TILES // 2 - 1, 1)
                norm2_b(TILES - 1, TILES // 2 - 1, 1)
            with dve.Else():
                dense_vector(dve, restart_chain, link, at)

        @block.tensor
        def _(pe):
            mm = nc.tensor.matmul

            def pack(t, half, b, halves):
                if 0 in halves:
                    pe.wait_ge(hit_ready, t + 1)
                    if not isinstance(t, int) or t >= 1:
                        pe.wait_ge(cand_done, t)
                for c in halves:
                    for k in range(FOLD):
                        lo = k * POS + c * 512
                        mm(ps_code[c][:, :], scaled_id[:, k, :], hit[:, b, lo:lo + 512], start=(k == 0), stop=False)
                    mm(ps_code[c][:, :], scaled_id[:, FOLD, :], 
                       pos_high[:, 2 * c:2 * c + 2].rearrange("p (n a) -> p n a", a=1).to_broadcast([P, 2, 256]),
                       start=False, stop=False)
                    last = mm(ps_code[c][:, :], scaled_id[:, FOLD + 1, :],
                              pos_low[:, :].rearrange("p (a n) -> p a n", a=1).to_broadcast([P, 2, 256]),
                              start=False, stop=True)
                if 1 in halves:
                    last.then_inc(packed, 1)

            def finish(t, half, b):
                pe.wait_ge(x1_ready, t + 1)
                if not isinstance(t, int) or t >= 1:
                    pe.wait_ge(wh_copied, t)
                nc.tensor.transpose(ps_wh[:, 0:P], x1[:, b, :], ident[:, :]).then_inc(x1T_ready, 1)
                pe.wait_ge(x1T_copied, t + 1)
                mm(ps_wh[:, 0:EXT], x1T[:, :], w_ext[:, :], start=True, stop=True).then_inc(wh_ready, 1)

            def back(t, half, b):
                pe.wait_ge(scored, t + 1)
                pe.wait_ge(maps_done, t + 1)
                back_sum(b, ps_back[:, 0:SPILL], SPILL).then_inc(back_ready, 1)

            def back_sum(b, dst, n):
                for c in range(BLOCKS):
                    last = mm(dst, to_row[:, b, c * P:(c + 1) * P], spread[:, c, 0:n], start=(c == 0),
                              stop=(c == BLOCKS - 1))
                return last

            def ends(t, half, b):
                pe.wait_ge(spill_n_ready, t + 1)
                mm(ps_end[:, 0:1], upper[:, 0, :], spill_n[:, :], start=True, stop=True)
                mm(ps_end[:, 1:2], upper[:, 1, :], spill_n[:, :], start=True, stop=True).then_inc(end_ready, 1)

            def maps(t, half, b):
                pe.wait_ge(map_ready, t + 1)
                for c in range(BLOCKS):
                    mm(ps_pick[:, c, :], to_spill[:, b, c * P:(c + 1) * P], cols[:, b, PRIMARY:SLOTS + 1], start=True,
                       stop=True)
                if not isinstance(t, int) or t >= 1:
                    pe.wait_ge(maps_done, t)
                for c in range(BLOCKS):
                    at_c = (b * BLOCKS + c) * D
                    mm(ps_xs[:, at_c:at_c + D], to_spill[:, b, c * P:(c + 1) * P],
                       x_sb[:, bass.ds(t, 1), :].rearrange("p a d -> p (a d)"), start=True, stop=True)
                turn_map(b).then_inc(mapT_ready, 1)

            def turn_map(b):
                for c in range(BLOCKS):
                    last = nc.tensor.transpose(ps_toT[:, c * P:(c + 1) * P], to_spill[:, b, c * P:(c + 1) * P], ident[:, :])
                return last

            def probs(t, half, b):
                pe.wait_ge(prob_ready, t + 1)
                for c in range(BLOCKS):
                    last = mm(ps_pf[:, c * SPILL:(c + 1) * SPILL], to_spill[:, b, c * P:(c + 1) * P],
                              prob[:, b, 0, PRIMARY:SLOTS], start=True, stop=True)
                last.then_inc(pf_ready, 1)

            def sum_rows(rows, b, done):
                for s in range(PRIMARY):
                    mm(ps_y[:, 0:D], ident[:, :], rows[:, s, 0:D], start=(s == 0), stop=False)
                for c in range(BLOCKS):
                    last = mm(ps_y[:, 0:D], to_row[:, b, c * P:(c + 1) * P], rows[:, PRIMARY + c, 0:D], start=False,
                              stop=(c == BLOCKS - 1))
                last.then_inc(done, 1)

            def weighted_sum(t, half, b):
                pe.wait_ge(weighted, t + 1)
                if not isinstance(t, int) or t >= 1:
                    pe.wait_ge(var_ready, t)
                sum_rows(weighed, b, y_ready)

            def step(t, half, b, lst=True, attend=True, end=True):
                prev, last = (t - 1, half - 1 + b, 1 - b), (t - 2, half - 1, b)
                more = not isinstance(t, int) or t < TILES - 2
                if lst:
                    ends(t, half, b)
                if end:
                    weighted_sum(*last)
                if lst:
                    maps(t, half, b)
                if more:
                    pack(t + 2, half + 1, b, (0,))
                if attend:
                    back(*prev)
                if more:
                    pack(t + 2, half + 1, b, (1,))
                if attend:
                    probs(*prev)
                if end:
                    finish(*last)

            pe.wait_ge(consts, 1)
            pe.wait_ge(w_ready, 1)
            pack(0, 0, 0, (0, 1))
            pack(1, 0, 1, (0, 1))
            pe.wait_ge(x_in, 16)
            step(0, 0, 0, attend=False, end=False)
            step(1, 0, 1, end=False)
            step(2, 1, 0)
            step(3, 1, 1)
            with pe.Fori(0, (TILES - 6) // 2) as q:
                for b in range(2):
                    step(q * 2 + (4 + b), q + 2, b)
            step(TILES - 2, TILES // 2 - 1, 0)
            step(TILES - 1, TILES // 2 - 1, 1)
            step(TILES, TILES // 2, 0, lst=False)
            step(TILES + 1, TILES // 2, 1, lst=False, attend=False)

            pe.wait_ge(bad_ready, 1)
            mm(ps_end[0:1, 0:1], bad_n[:, :], ones[:, 0:1], start=True, stop=True).then_inc(bad_summed, 1)

            with pe.If(sparse(pe) == 0):
                def maps2(t, half, b):
                    pe.wait_ge(T["map_ready"], t + 1)
                    if not isinstance(t, int) or t >= 1:
                        pe.wait_ge(T["mapT_copied"], t)
                    turn_map(b).then_inc(T["mapT_ready"], 1)

                def back2(t, half, b):
                    pe.wait_ge(T["spread_ready"], t + 1)
                    pe.wait_ge(T["mapT_copied"], t + 1)
                    back_sum(b, ps_back[:, 0:H * SPILL], H * SPILL).then_inc(T["back_ready"], 1)

                def probs2(t, half, b):
                    pe.wait_ge(T["prob_ready"], t + 1)
                    for c in range(BLOCKS):
                        last = mm(ps_pf[:, c * H * SPILL:(c + 1) * H * SPILL], to_spill[:, b, c * P:(c + 1) * P],
                                  prob[:, b, :, PRIMARY:SLOTS], start=True, stop=True)
                    last.then_inc(T["pf_ready"], 1)

                def step2(t, half, b, maps=True, attend=True, end=True):
                    prev = (t - 1, half - 1 + b, 1 - b)
                    if maps:
                        maps2(t, half, b)
                    if attend:
                        back2(*prev)
                        probs2(*prev)
                        pe.wait_ge(T["weighted"], prev[0] + 1)
                        if not isinstance(t, int) or t >= 2:
                            pe.wait_ge(T["low_ready"], t - 1)
                        sum_rows(keys[:, 1 - b, :, :], 1 - b, T["y_ready"])

                step2(0, 0, 0, attend=False)
                step2(1, 0, 1)
                step2(2, 1, 0)
                step2(3, 1, 1)
                tiles_of(pe, step2)
                step2(TILES, TILES // 2, 0, maps=False)
            with pe.Else():
                dense_tensor(pe)

_INS = ["x", "adj", "L0_gnn_ks", "L1_gnn_W", "L1_gnn_a"]


def kernel(**inputs):
    import numpy as np
    import concourse.bacc as bacc
    from concourse.bass_utils import run_bass_kernel_spmd as run

    nc = bacc.Bacc("TRN2", target_bir_lowering=False, num_devices=1)
    arrays, args = {}, []
    for name in _INS:
        v = np.ascontiguousarray(inputs[name])
        arrays[f"in_{name}_dram"] = v
        args.append(nc.dram_tensor(f"in_{name}_dram", v.shape, mybir.dt.from_np(v.dtype), kind="ExternalInput").ap())
    out = nc.dram_tensor("out_dram", inputs["x"].shape, F32, kind="ExternalOutput").ap()
    adj_resnorm_kernel(nc, *args, out)
    return run(nc, [arrays], core_ids=[0]).results[0]["out_dram"]
```
